# Optimizing a Trainium2 kernel written in Bass

```python
import numpy as np
import jax
import jax.numpy as jnp

def _softmax(x, axis=-1):
    return jax.nn.softmax(x, axis=axis)

def _gelu(x):
    return jax.nn.gelu(x, approximate=True)

def _silu(x):
    return jax.nn.silu(x)

def _sigmoid(x):
    return jax.nn.sigmoid(x)

def _layernorm(x, axis=-1, eps=1e-05):
    m = jnp.mean(x, axis=axis, keepdims=True)
    v = jnp.var(x, axis=axis, keepdims=True)
    return (x - m) / jnp.sqrt(v + eps)

def _scatter_add(tgt, idx, src, axis=0):
    return tgt.at[idx].add(src)

def _segment_sum(src, seg, n):
    return jax.ops.segment_sum(src, seg, n)
kernel_name = 'mk_flamingo_gated_d1_seqx_r4_0a0707'

def setup_inputs(seed: int=0):
    np.random.seed(seed)
    _w = jnp.asarray

    def _rec_inputs():
        import jax
        import jax.numpy as jnp
        _rk = jax.random.key(seed)
        x = 7.22e-05 + 1 * jax.random.normal(jax.random.fold_in(_rk, 1), (4, 1024, 256), jnp.float32)
        _lenS = 1024 - jax.random.randint(jax.random.fold_in(_rk, 7), (4,), 0, max(1, 1024 // 4) + 1, jnp.int32)
        _lenS2 = 154 - jax.random.randint(jax.random.fold_in(_rk, 8), (4,), 0, max(1, 154 // 4) + 1, jnp.int32)
        _ctx_768P = jax.random.normal(jax.random.fold_in(_rk, 11), (4, 16, 192), jnp.float32)
        _ctx_768c = jax.random.dirichlet(jax.random.fold_in(_rk, 511), 0.3 * jnp.ones((16,), jnp.float32), (4, 154))
        _ctx_768t = jnp.einsum('bsk,bkd->bsd', _ctx_768c, _ctx_768P)
        _ctx_768t = _ctx_768t * jax.lax.rsqrt(jnp.mean(jnp.square(_ctx_768t)) + 1e-12) * 0.953939
        ctx_768 = -0.000191848 + 0.999787 * (_ctx_768t + 0.3 * jax.random.normal(jax.random.fold_in(_rk, 611), (4, 154, 192), jnp.float32))
        _validS = jnp.arange(1024)[None, :] < _lenS[:, None]
        _validS2 = jnp.arange(154)[None, :] < _lenS2[:, None]
        _causal = jnp.tril(jnp.ones((1024, 1024), dtype=bool))
        mask_BxS2_bk0 = jnp.logical_not(jnp.broadcast_to(_validS2[:, :], (4, 154)))
        _g = jax.random.normal(jax.random.fold_in(_rk, 9001), (2, 1), jnp.float32)
        _g = jnp.sign(_g) * jnp.maximum(jnp.abs(_g), 1.0) + (_g == 0) * 1.0
        g_xattn = _g[0]
        g_ffn = _g[1]
        return (x, ctx_768, mask_BxS2_bk0, g_xattn, g_ffn)
    x, ctx_768, mask_BxS2_bk0, g_xattn, g_ffn = _rec_inputs()

    def _L0_xattn_setup():
        import jax, jax.numpy as jnp
        import numpy as np
        HEADS = 8
        DIM_HEAD = 64
        QUERY_DIM = 256
        CONTEXT_DIM = 192
        INNER = HEADS * DIM_HEAD
        key = jax.random.key(seed)
        ks = jax.random.split(key, 8)
        b, n, j = (4, 512, 512)
        x = jax.random.normal(ks[0], (b, n, QUERY_DIM), dtype=jnp.float32)
        context = jax.random.normal(ks[1], (b, j, CONTEXT_DIM), dtype=jnp.float32)
        mask = jax.random.randint(ks[2], (b, j), 0, 2).astype(jnp.bool_)
        W_q = jax.random.normal(ks[3], (QUERY_DIM, INNER), dtype=jnp.float32) / np.sqrt(QUERY_DIM)
        W_k = jax.random.normal(ks[4], (CONTEXT_DIM, INNER), dtype=jnp.float32) / np.sqrt(CONTEXT_DIM)
        W_v = jax.random.normal(ks[5], (CONTEXT_DIM, INNER), dtype=jnp.float32) / np.sqrt(CONTEXT_DIM)
        W_o = jax.random.normal(ks[6], (INNER, QUERY_DIM), dtype=jnp.float32) / np.sqrt(INNER)
        b_o = jax.random.normal(ks[7], (QUERY_DIM,), dtype=jnp.float32) * 0.01
        return {'x': x, 'context': context, 'mask': mask, 'W_q': W_q, 'W_k': W_k, 'W_v': W_v, 'W_o': W_o, 'b_o': b_o}
    _L0_xattn_all = _L0_xattn_setup()
    _L0_xattn_in = {k: v for k, v in _L0_xattn_all.items() if k in ('W_q', 'W_k', 'W_v', 'W_o', 'b_o')}
    del _L0_xattn_all

    def _L0_ffn_setup():
        import jax, jax.numpy as jnp
        import numpy as np
        HIDDEN = 256
        MOE_INTER = 128
        SHARED_INTER = 512
        N_EXPERTS = 32
        TOP_K = 6
        N_GROUP = 8
        TOPK_GROUP = 4
        ROUTED_SCALE = 2.5

        def _relu2(x):
            return jnp.square(jax.nn.relu(x))

        def _router(x, gate_w, e_bias):
            T = x.shape[0]
            logits = x.astype(jnp.float32) @ gate_w.astype(jnp.float32).T
            scores = jax.nn.sigmoid(logits)
            sc = scores + e_bias[None, :]
            g = sc.reshape(T, N_GROUP, N_EXPERTS // N_GROUP)
            group_scores = jax.lax.top_k(g, 2)[0].sum(-1)
            group_idx = jax.lax.top_k(group_scores, TOPK_GROUP)[1]
            group_mask = jnp.zeros_like(group_scores).at[jnp.arange(T)[:, None], group_idx].set(1.0)
            score_mask = jnp.repeat(group_mask, N_EXPERTS // N_GROUP, axis=1)
            masked = jnp.where(score_mask > 0, sc, 0.0)
            topk_idx = jax.lax.stop_gradient(jax.lax.top_k(masked, TOP_K)[1])
            topk_w = jnp.take_along_axis(scores, topk_idx, axis=1)
            topk_w = topk_w / (topk_w.sum(-1, keepdims=True) + 1e-20)
            topk_w = topk_w * ROUTED_SCALE
            return (topk_idx, topk_w)
        if __name__ == '__main__':
            out = reference(**setup_inputs())
            print(out.shape, out.dtype)
        key = jax.random.key(seed)
        ks = jax.random.split(key, 6)
        s = 0.02
        return {'hidden_states': jax.random.normal(ks[0], (2, 256, HIDDEN), jnp.float32), 'gate_w': jax.random.normal(ks[1], (N_EXPERTS, HIDDEN), jnp.float32) * s, 'e_bias': jnp.zeros((N_EXPERTS,), jnp.float32), 'up_w': jax.random.normal(ks[2], (N_EXPERTS, MOE_INTER, HIDDEN), jnp.float32) * s, 'down_w': jax.random.normal(ks[3], (N_EXPERTS, HIDDEN, MOE_INTER), jnp.float32) * s, 'shared_up_w': jax.random.normal(ks[4], (SHARED_INTER, HIDDEN), jnp.float32) * s, 'shared_down_w': jax.random.normal(ks[5], (HIDDEN, SHARED_INTER), jnp.float32) * s}
    _L0_ffn_all = _L0_ffn_setup()
    _L0_ffn_in = {k: v for k, v in _L0_ffn_all.items() if k in ('gate_w', 'e_bias', 'up_w', 'down_w', 'shared_up_w', 'shared_down_w')}
    del _L0_ffn_all
    return {'x': x, 'ctx_768': ctx_768, 'mask_BxS2_bk0': mask_BxS2_bk0, 'g_xattn': g_xattn, 'g_ffn': g_ffn, 'L0_xattn_W_q': _L0_xattn_in['W_q'], 'L0_xattn_W_k': _L0_xattn_in['W_k'], 'L0_xattn_W_v': _L0_xattn_in['W_v'], 'L0_xattn_W_o': _L0_xattn_in['W_o'], 'L0_xattn_b_o': _L0_xattn_in['b_o'], 'L0_ffn_gate_w': _L0_ffn_in['gate_w'], 'L0_ffn_e_bias': _L0_ffn_in['e_bias'], 'L0_ffn_up_w': _L0_ffn_in['up_w'], 'L0_ffn_down_w': _L0_ffn_in['down_w'], 'L0_ffn_shared_up_w': _L0_ffn_in['shared_up_w'], 'L0_ffn_shared_down_w': _L0_ffn_in['shared_down_w']}

def reference(x, ctx_768, mask_BxS2_bk0, g_xattn, g_ffn, L0_xattn_W_q, L0_xattn_W_k, L0_xattn_W_v, L0_xattn_W_o, L0_xattn_b_o, L0_ffn_gate_w, L0_ffn_e_bias, L0_ffn_up_w, L0_ffn_down_w, L0_ffn_shared_up_w, L0_ffn_shared_down_w):
    import jax
    import jax.numpy as jnp

    def _L0_xattn_ref(x, context, mask, W_q, W_k, W_v, W_o, b_o):
        import jax, jax.numpy as jnp
        import numpy as np
        HEADS = 8
        DIM_HEAD = 64
        QUERY_DIM = 256
        CONTEXT_DIM = 192
        INNER = HEADS * DIM_HEAD
        b, n, _ = x.shape
        j = context.shape[1]
        scale = DIM_HEAD ** (-0.5)
        q = (x @ W_q).reshape(b, n, HEADS, DIM_HEAD)
        k = (context @ W_k).reshape(b, j, HEADS, DIM_HEAD)
        v = (context @ W_v).reshape(b, j, HEADS, DIM_HEAD)
        sim = jnp.einsum('bihd,bjhd->bhij', q, k) * scale
        max_neg = -jnp.finfo(sim.dtype).max
        sim = jnp.where(mask[:, None, None, :], sim, max_neg)
        attn = jax.nn.softmax(sim, axis=-1)
        out = jnp.einsum('bhij,bjhd->bihd', attn, v).reshape(b, n, INNER)
        return out @ W_o + b_o

    def _L0_ffn_ref(hidden_states, gate_w, e_bias, up_w, down_w, shared_up_w, shared_down_w):
        import jax, jax.numpy as jnp
        import numpy as np
        HIDDEN = 256
        MOE_INTER = 128
        SHARED_INTER = 512
        N_EXPERTS = 32
        TOP_K = 6
        N_GROUP = 8
        TOPK_GROUP = 4
        ROUTED_SCALE = 2.5

        def _relu2(x):
            return jnp.square(jax.nn.relu(x))

        def _router(x, gate_w, e_bias):
            T = x.shape[0]
            logits = x.astype(jnp.float32) @ gate_w.astype(jnp.float32).T
            scores = jax.nn.sigmoid(logits)
            sc = scores + e_bias[None, :]
            g = sc.reshape(T, N_GROUP, N_EXPERTS // N_GROUP)
            group_scores = jax.lax.top_k(g, 2)[0].sum(-1)
            group_idx = jax.lax.top_k(group_scores, TOPK_GROUP)[1]
            group_mask = jnp.zeros_like(group_scores).at[jnp.arange(T)[:, None], group_idx].set(1.0)
            score_mask = jnp.repeat(group_mask, N_EXPERTS // N_GROUP, axis=1)
            masked = jnp.where(score_mask > 0, sc, 0.0)
            topk_idx = jax.lax.stop_gradient(jax.lax.top_k(masked, TOP_K)[1])
            topk_w = jnp.take_along_axis(scores, topk_idx, axis=1)
            topk_w = topk_w / (topk_w.sum(-1, keepdims=True) + 1e-20)
            topk_w = topk_w * ROUTED_SCALE
            return (topk_idx, topk_w)
        if __name__ == '__main__':
            out = reference(**setup_inputs())
            print(out.shape, out.dtype)
        B, S, H = hidden_states.shape
        x = hidden_states.reshape(-1, H)
        T = x.shape[0]
        topk_idx, topk_w = _router(x, gate_w, e_bias)
        combine = jnp.zeros((T, N_EXPERTS), topk_w.dtype).at[jnp.arange(T)[:, None], topk_idx].add(topk_w)
        h = _relu2(jnp.einsum('th,eih->tei', x, up_w))
        h = h * combine[:, :, None]
        moe_out = jnp.einsum('tei,ehi->th', h, down_w)
        shared = _relu2(x @ shared_up_w.T) @ shared_down_w.T
        return (moe_out + shared).reshape(B, S, H)
    x = x + jnp.tanh(g_xattn[0]) * _L0_xattn_ref(_layernorm(x, axis=-1), ctx_768, mask_BxS2_bk0, L0_xattn_W_q, L0_xattn_W_k, L0_xattn_W_v, L0_xattn_W_o, L0_xattn_b_o)
    x = x + jnp.tanh(g_ffn[0]) * _L0_ffn_ref(_layernorm(x, axis=-1), L0_ffn_gate_w, L0_ffn_e_bias, L0_ffn_up_w, L0_ffn_down_w, L0_ffn_shared_up_w, L0_ffn_shared_down_w)
    return x

_drawn_inputs = setup_inputs


def setup_inputs(seed=0):
    import zlib

    import numpy as np

    out = dict(_drawn_inputs(seed))
    spreads = {'L0_ffn_e_bias': (0.0, 0.374)}
    factors = {'L0_xattn_b_o': 8.0, 'L0_ffn_gate_w': 3.297, 'L0_ffn_up_w': 2.71}
    for name, (base, spread) in spreads.items():
        noise = np.random.default_rng([zlib.crc32(name.encode()), seed]).standard_normal(out[name].shape)
        drawn = base * np.exp(spread * noise) if base else spread * noise
        out[name] = jnp.asarray(drawn.astype(out[name].dtype))
    for name, factor in factors.items():
        out[name] = (out[name] * factor).astype(out[name].dtype)
    return out
```

```python
from contextlib import ExitStack

import concourse.bass as bass
from concourse import mybir

F32 = mybir.dt.float32
F32R = mybir.dt.float32r
BF16 = mybir.dt.bfloat16
I32 = mybir.dt.int32
U32 = mybir.dt.uint32
U8 = mybir.dt.uint8
ALU = mybir.AluOpType
ACT = mybir.ActivationFunctionType
AX_X = mybir.AxisListType.X

P = 128
EPS = 1e-5
BIG = 3.0e38
RSQRT_MAGIC = 1597463007.0
ROUTED_SCALE = 2.5


def flamingo_block(nc, x, ctx_t, mask, g_xattn, g_ffn, w_q, w_k, w_v, w_o, b_o, gate_t, e_bias,
                   w_moe, eye, iota, out):
    n_tok, D = x.shape
    NB, CD, J = ctx_t.shape
    INNER = w_q.shape[1]
    DH = 64
    NH = INNER // DH
    SCALE = float(DH) ** -0.5
    KC = D // P
    MC = INNER // P
    NE = e_bias.shape[0]
    NG, GE, TOPG, TOPK = 8, NE // 8, 4, 6
    NX = w_moe.shape[1]
    EW = KC * P
    BT = 512
    TB = BT // P
    N_BLK = n_tok // BT
    XT = NX // TB
    BLK_B = n_tok // NB // BT
    BANK_H = (3, 3, 2)
    HJ = NH * J
    NCH = -(-HJ // P)
    AV = [(m, c) for m in range(MC) for c in range(NCH)
          if c * P < (2 * m + 2) * J and (c + 1) * P > 2 * m * J]
    NAV = len(AV)
    WIN = P + J + P
    RING = 3
    assert XT % RING == 0 and NX == TB * XT

    x_tiles = x.rearrange("(t p) d -> t p d", p=P)
    out_blk = out.rearrange("(b t p) d -> b p t d", p=P, t=TB)
    comb_dram = nc.dram_tensor("combine_weights", [NX, n_tok], F32, kind="Internal").ap()
    kd_hi = nc.dram_tensor("keys_hi", [NB, P, NH * J], F32, kind="Internal").ap()
    kd_lo = nc.dram_tensor("keys_lo", [NB, P, NH * J], F32, kind="Internal").ap()
    vd_hi = nc.dram_tensor("values_hi", [NB, P, NAV * P], F32, kind="Internal").ap()
    vd_lo = nc.dram_tensor("values_lo", [NB, P, NAV * P], F32, kind="Internal").ap()

    with ExitStack() as ctx:
        def sb(name, shape, dt):
            return ctx.enter_context(nc.sbuf_tensor(name, shape, dt))

        def sem(name):
            return ctx.enter_context(nc.semaphore(name))

        ps = ctx.enter_context(nc.psum_tensor("ps", [P, 8, 512], F32))
        acc = ps[:, 0:2, :]
        hid = ps[:, 2:5, :]
        att = ps[:, 5:8, :]

        w_raw = sb("w_raw", [P, NX, 2 * EW], F32)
        wu_hi = sb("wu_hi", [P, RING, EW], F32R)
        wu_lo = sb("wu_lo", [P, RING, EW], F32R)
        wd_hi = sb("wd_hi", [P, RING, EW], F32R)
        wd_lo = sb("wd_lo", [P, RING, EW], F32R)
        wq_hi = sb("wq_hi", [P, KC * INNER], F32R)
        wq_lo = sb("wq_lo", [P, KC * INNER], F32R)
        wo_hi = sb("wo_hi", [P, MC * D], F32R)
        wo_lo = sb("wo_lo", [P, MC * D], F32R)
        gate_hi = sb("gate_hi", [P, KC, P], F32R)
        gate_lo = sb("gate_lo", [P, KC, P], F32R)
        k_hi = sb("k_hi", [P, NH, J], F32R)
        k_lo = sb("k_lo", [P, NH, J], F32R)
        v_hi = sb("v_hi", [P, NAV * P], F32R)
        v_lo = sb("v_lo", [P, NAV * P], F32R)
        ident = sb("ident", [P, P], F32)
        iota_f = sb("iota_f", [P, NE], F32)
        bias_e = sb("bias_e", [P, NE], F32)
        bias_o = sb("bias_o", [P, D], F32)
        gates = sb("gates", [P, 2], F32)
        tanh_g = sb("tanh_g", [P, 2], F32)
        mask_u8 = sb("mask_u8", [P, NB, J], U8)
        mask_add = sb("mask_add", [P, NB, J], BF16)
        row0 = sb("row0", [P, P], BF16)
        ones = sb("ones", [P, EW], F32)
        ones_row = sb("ones_row", [NX - NE, 512], F32)
        gate_raw = sb("gate_raw", [P, KC, NE], F32)
        x_in = sb("x_in", [P, D], F32)
        x_n = sb("x_n", [P, D], F32)
        x1t_hi = sb("x1t_hi", [P, EW], F32R)
        x1t_lo = sb("x1t_lo", [P, EW], F32R)
        q_hi = sb("q_hi", [P, INNER], F32R)
        q_lo = sb("q_lo", [P, INNER], F32R)
        prob = sb("prob", [P, NCH * P], F32)
        pt_hi = sb("pt_hi", [P, NCH * P], F32R)
        pt_lo = sb("pt_lo", [P, NCH * P], F32R)
        at_hi, at_lo = q_hi, q_lo
        nmax = sb("nmax", [P, NH], F32)
        psum_exp = sb("psum_exp", [P, NH], F32)
        rsum = sb("rsum", [P, NH], F32)
        ln_s = sb("ln_s", [P, 16], F32)
        ln_i = sb("ln_i", [P, 2], I32)
        x1 = sb("x1", [P, 2, TB, D], F32)
        x2t_hi = sb("x2t_hi", [P, 2, KC, BT], F32R)
        x2t_lo = sb("x2t_lo", [P, 2, KC, BT], F32R)
        lt_sb = sb("lt_sb", [P, P], F32)
        exp_l = sb("exp_l", [P, NE], F32)
        score = sb("score", [P, NE], F32)
        biased = sb("biased", [P, NE], F32)
        grp = sb("grp", [P, 96], F32)
        grp_i = sb("grp_i", [P, 16], U32)
        hot_g = sb("hot_g", [P, TOPG, NG], F32)
        masked = sb("masked", [P, NE], F32)
        hot = sb("hot", [P, TOPK, NE], F32)
        sel = sb("sel", [P, NE], F32)
        weighted = sb("weighted", [P, NE], F32)
        comb = sb("comb", [P, P], F32)
        comb_t = sb("comb_t", [NE, P], F32)
        comb_b = sb("comb_b", [P, RING, BT], F32)
        act_f = sb("act_f", [P, RING, BT], F32)
        act_hi = sb("act_hi", [P, RING, BT], F32R)
        act_lo = sb("act_lo", [P, RING, BT], F32R)
        y_t = act_f[:, 0:KC, :]

        raw_a = act_f[:, :, :].rearrange("p a b -> p (a b)")
        raw_b = comb_b[:, :, :].rearrange("p a b -> p (a b)")
        raw_c = x1[:, :, :, :].rearrange("p a t d -> p (a t d)")
        ctx_raw = prob[:, 0:NB * 2 * J].rearrange("p (b c j) -> p b c j", b=NB, c=2)
        wk_hi = act_hi[:, :, :].rearrange("p a b -> p (a b)")[:, 0:2 * INNER]
        wk_lo = act_lo[:, :, :].rearrange("p a b -> p (a b)")[:, 0:2 * INNER]
        wv_hi = x2t_hi[:, 1, :, :].rearrange("p a b -> p (a b)")
        wv_lo = x2t_lo[:, 1, :, :].rearrange("p a b -> p (a b)")
        win_hi = x2t_hi[:, 0, :, :].rearrange("p a b -> p (a b)")[:, 0:2 * WIN].rearrange("p (c w) -> p c w", c=2)
        win_lo = x2t_lo[:, 0, :, :].rearrange("p a b -> p (a b)")[:, 0:2 * WIN].rearrange("p (c w) -> p c w", c=2)

        s_zero = sem("rows_cleared")
        s_const = sem("constants_loaded")
        s_wa = sem("attention_weights_loaded")
        s_wm = sem("expert_weights_loaded")
        s_ones = sem("ones_ready")
        s_mask = sem("mask_ready")
        s_tanh = sem("tanh_ready")
        s_split = sem("attention_weights_split")
        s_win = sem("context_split")
        s_kvp = sem("keys_values_in_psum")
        s_kvh = sem("keys_values_hi")
        s_kvl = sem("keys_values_lo")
        s_kvs = sem("keys_values_stored")
        s_x = sem("x_loaded")
        s_kv = sem("keys_values_loaded")
        s_xn = sem("normed")
        s_xt = sem("normed_t_psum")
        s_xth = sem("normed_t_hi")
        s_xtl = sem("normed_t_lo")
        s_q = sem("q_psum")
        s_qh = sem("q_hi_ready")
        s_ql = sem("q_lo_ready")
        s_s = sem("scores_psum")
        s_nm = sem("max_ready")
        s_p = sem("exp_ready")
        s_pn = sem("prob_ready")
        s_pt = sem("prob_t_psum")
        s_pth = sem("prob_t_hi")
        s_ptl = sem("prob_t_lo")
        s_a = sem("heads_psum")
        s_ah = sem("heads_hi")
        s_al = sem("heads_lo")
        s_o = sem("attn_out_psum")
        s_x1 = sem("residual_ready")
        s_lt = sem("logits_t_psum")
        s_lts = sem("logits_t_sbuf")
        s_l = sem("logits_psum")
        s_e = sem("logits_exp")
        s_c = sem("combine_ready")
        s_ct = sem("combine_t_psum")
        s_cts = sem("combine_t_sbuf")
        s_cd = sem("combine_stored")
        s_wu = sem("up_staged")
        s_wd = sem("down_staged")
        s_cb = [sem(f"combine_row_{i}") for i in range(RING)]
        s_up = sem("hidden_psum")
        s_sq = sem("squared")
        s_g = sem("weighted_hidden")
        s_gh = sem("hidden_hi")
        s_gl = sem("hidden_lo")
        s_dn = sem("down_done")
        s_y = sem("sum_t_sbuf")
        s_yt = sem("sum_psum")
        s_out = sem("output_ready")
        s_st = sem("output_stored")
        s_x1free = sem("residual_free")

        block = ctx.enter_context(nc.Block())

        def three(o, l_hi, l_lo, r_hi, r_lo, start, stop):
            nc.tensor.matmul(o, l_hi, r_lo, start=start, stop=False, skip_group_check=True)
            nc.tensor.matmul(o, l_lo, r_hi, start=False, stop=False, skip_group_check=True)
            return nc.tensor.matmul(o, l_hi, r_hi, start=False, stop=stop, skip_group_check=True)


        @block.sync
        def _(sp):
            sp.sem_inc(s_x1free, 1)
            for dst, src in ((ident[:], eye), (iota_f[:], iota),
                             (bias_e[:], e_bias.partition_broadcast(P)),
                             (bias_o[:], b_o.partition_broadcast(P)),
                             (gates[:, 0:1], g_xattn.partition_broadcast(P)),
                             (gates[:, 1:2], g_ffn.partition_broadcast(P)),
                             (gate_raw[:], gate_t.rearrange("(c p) e -> p c e", p=P))):
                sp.dma_start(dst, src).then_inc(s_const, 16)
            sp.wait_ge(s_zero, 1)
            sp.dma_start(mask_u8[0:1, :, :], mask.rearrange("(a b) j -> a b j", a=1)).then_inc(s_const, 16)
            half = CD - P
            for dst, src in (
                (raw_a[:, 0:INNER], w_k[0:P, :]), (raw_a[0:half, INNER:2 * INNER], w_k[P:CD, :]),
                (raw_b[:, 0:INNER], w_v[0:P, :]), (raw_b[0:half, INNER:2 * INNER], w_v[P:CD, :]),
                (ctx_raw[:, :, 0, :], ctx_t[:, 0:P, :].rearrange("b p j -> p b j")),
                (ctx_raw[0:half, :, 1, :], ctx_t[:, P:CD, :].rearrange("b p j -> p b j")),
                (raw_c[:, 0:KC * INNER].rearrange("p (c n) -> p c n", c=KC), w_q.rearrange("(c p) n -> p c n", p=P)),
            ):
                sp.dma_start(dst, src).then_inc(s_wa, 16)
            sp.wait_ge(s_split, 1)
            sp.dma_start(raw_a[:, 0:MC * D].rearrange("p (c n) -> p c n", c=MC),
                         w_o.rearrange("(c p) n -> p c n", p=P)).then_inc(s_wa, 16)
            sp.wait_ge(s_ones, 1)
            sp.dma_start(comb_dram[NE:NX, :].rearrange("e (a n) -> e a n", n=512),
                         ones_row[:, :].unsqueeze(1).broadcast_to([NX - NE, n_tok // 512, 512])).then_inc(s_cd, 16)
            with sp.Fori(0, NB) as b:
                sp.wait_ge(s_kvl, 6 * b + 12)
                for dst, src in ((kd_hi, k_hi[:, :, :].rearrange("p a b -> p (a b)")),
                                 (kd_lo, k_lo[:, :, :].rearrange("p a b -> p (a b)")),
                                 (vd_hi, v_hi[:]), (vd_lo, v_lo[:])):
                    sp.dma_start(dst[b], src.bitcast(F32)).then_inc(s_kvs, 16)
            sp.wait_ge(s_kvs, 64 * NB)
            for e0 in range(0, NX, 12):
                sp.dma_start(w_raw[:, e0:e0 + 12, :], w_moe[:, e0:e0 + 12, :]).then_inc(s_wm, 16)

            def load_context(b):
                for dst, src in ((k_hi[:, :, :].rearrange("p a b -> p (a b)"), kd_hi),
                                 (k_lo[:, :, :].rearrange("p a b -> p (a b)"), kd_lo),
                                 (v_hi[:], vd_hi), (v_lo[:], vd_lo)):
                    sp.dma_start(dst.bitcast(F32), src[b]).then_inc(s_kv, 16)

            def load_x(T):
                sp.wait_ge(s_x1, T + 1)
                sp.dma_start(x_in[:], x_tiles[T]).then_inc(s_x, 16)

            def store_combine(T):
                sp.wait_ge(s_cts, T + 2)
                sp.wait_ge(s_cd, 16 * T + 16)
                sp.dma_start(comb_dram[0:NE, bass.ds(T * P, P)], comb_t[:]).then_inc(s_cd, 16)

            def load_row(B, t, k):
                X = NX * B + XT * t + k
                sp.wait_ge(s_g, X + 1)
                sp.dma_start(comb_b[:, k % RING, :],
                             comb_dram[XT * t + k, bass.ds(B * BT, BT)].partition_broadcast(P)
                             ).then_inc(s_cb[k % RING], 16)

            def tile_step(B, t, first, attend):
                T = TB * (B + 1) + t
                if attend:
                    load_x(T)
                for k in range(XT):
                    load_row(B, t, k)
                    if attend and k == 2 and not first:
                        store_combine(T - 1)

            def store_block(B):
                sp.wait_ge(s_out, 2 * B + 4)
                sp.dma_start(out_blk[B], x1[:, bass.ds(B % 2, 1), :, :].rearrange("p a t d -> p (a t) d")
                             ).then_inc(s_st, 16)
                sp.wait_ge(s_st, 16 * B + 16)
                sp.sem_inc(s_x1free, 1)

            load_context(0)
            with sp.Fori(0, TB) as t:
                load_x(t)
                store_combine(t)

            def moe_block(B, attend):
                if attend:
                    b = sp.snap((B + 1) // BLK_B)
                    sp.wait_ge(s_a, TB * B + TB)
                    load_context(b)
                sp.wait_ge(s_cd, 16 * (TB * B + TB) + 16)
                tile_step(B, 0, True, attend)
                with sp.Fori(1, TB) as t:
                    tile_step(B, t, False, attend)
                if attend:
                    store_combine(TB * (B + 1) + TB - 1)
                store_block(B)

            with sp.Fori(0, N_BLK - 1) as B:
                moe_block(B, True)
            moe_block(N_BLK - 1, False)

        @block.gpsimd
        def _(pool):
            nc.gpsimd.memset(ones[:], 1.0)
            pool.drain()
            pool.wait_ge(s_wm, 16 * 3)

            def stage(X, e, k, first_col, hi, lo, s_free, s_lo):
                raw = w_raw[:, bass.ds(e, 1), first_col:first_col + EW].rearrange("p a n -> p (a n)")
                r = k % RING
                pool.wait_ge(s_free, X + 1)
                nc.gpsimd.tensor_tensor(hi[:, r, :], raw, ones[:], ALU.mult)
                pool.drain()
                nc.gpsimd.tensor_tensor(lo[:, r, :], raw, hi[:, r, :].bitcast(F32), ALU.subtract).then_inc(s_lo, 1)

            with pool.Fori(0, N_BLK) as B:
                with pool.Fori(0, TB) as t:
                    for k in range(XT):
                        X = NX * B + XT * t + k
                        stage(X, XT * t + k, k, 0, wu_hi, wu_lo, s_up, s_wu)
                        stage(X, XT * t + k, k, EW, wd_hi, wd_lo, s_dn, s_wd)

        @block.scalar
        def _(act):
            act.wait_ge(s_const, 16 * 8)
            nc.scalar.activation(tanh_g[:], gates[:], ACT.Tanh).then_inc(s_tanh, 1)
            with act.Fori(0, NB) as b:
                act.wait_ge(s_kvp, 2 * b + 3)
                for m in range(MC):
                    src = ps[:, m // 3, (m % 3) * J:(m % 3 + 1) * J]
                    nc.scalar.activation(k_hi[0:64, 2 * m, :], src[0:64, :], ACT.Copy)
                    i = nc.scalar.activation(k_hi[64:P, 2 * m + 1, :], src[64:P, :], ACT.Copy)
                    if m >= 2:
                        i.then_inc(s_kvh, 1)
                act.wait_ge(s_kvp, 2 * b + 4)
                for j in range(4):
                    n = min(4, NAV - 4 * j) * P
                    nc.scalar.activation(v_hi[:, 512 * j:512 * j + n], ps[:, 2 + j, 0:n], ACT.Copy).then_inc(s_kvh, 1)

            act.sem_inc(s_cts, 1)

            def normed_t(T, ln):
                n = 2 * T + ln + 1
                act.wait_ge(s_xt, n)
                if ln == 0:
                    nc.scalar.activation(x1t_hi[:], att[:, 0, 0:EW], ACT.Copy).then_inc(s_xth, 1)
                else:
                    dst = x2t_hi[:, bass.ds(T // TB % 2, 1), :, bass.ds(T % TB * P, P)].rearrange("p a c n -> p (a c) n")
                    nc.scalar.activation(dst, att[:, 2, 0:EW].rearrange("p (c n) -> p c n", c=KC), ACT.Copy).then_inc(s_xth, 1)

            def q_part(T):
                act.wait_ge(s_q, T + 1)
                nc.scalar.activation(q_hi[:], att[:, 1, :], ACT.Copy).then_inc(s_qh, 1)

            def exps(T):
                h = 0
                for bank, nh in enumerate(BANK_H):
                    act.wait_ge(s_nm, 3 * T + bank + 1)
                    for i in range(nh):
                        ins = nc.scalar.activation(prob[:, h * J:(h + 1) * J], att[:, bank, i * J:(i + 1) * J], ACT.Exp,
                                                   bias=nmax[:, h:h + 1], scale=SCALE, accum_out=psum_exp[:, h:h + 1])
                        h += 1
                    ins.then_inc(s_p, 1)

            def prob_t(T):
                for bank in range(3):
                    n = min(4, NCH - 4 * bank) * P
                    act.wait_ge(s_pt, 3 * T + bank + 1)
                    nc.scalar.activation(pt_hi[:, 512 * bank:512 * bank + n], att[:, bank, 0:n], ACT.Copy).then_inc(s_pth, 1)

            def heads(T):
                act.wait_ge(s_a, T + 1)
                nc.scalar.activation(at_hi[:], att[:, 0, :], ACT.Copy).then_inc(s_ah, 1)

            def logits_t(T):
                act.wait_ge(s_lt, T + 1)
                nc.scalar.activation(lt_sb[:], att[:, 1, 256:384], ACT.Copy).then_inc(s_lts, 1)

            def logits_exp(T):
                act.wait_ge(s_l, T + 1)
                nc.scalar.activation(exp_l[:], att[:, 1, 384:384 + NE], ACT.Exp, scale=-1.0).then_inc(s_e, 1)

            def combine_t(T):
                act.wait_ge(s_ct, T + 1)
                act.wait_ge(s_cd, 16 * T + 16)
                nc.scalar.activation(comb_t[:], att[0:NE, 2, 256:384], ACT.Copy).then_inc(s_cts, 1)

            def hidden_hi(X, k):
                act.wait_ge(s_g, X + 4)
                nc.scalar.activation(act_hi[:, k % RING, :], act_f[:, k % RING, :], ACT.Copy).then_inc(s_gh, 1)

            def hidden(X, k):
                a = act_f[:, k % RING, :]
                act.wait_ge(s_up, X + 4)
                nc.scalar.activation(a, hid[:, k % RING, :], ACT.Relu)
                act.drain()
                nc.scalar.activation(a, a, ACT.Square).then_inc(s_sq, 1)

            def tile_step(B, t, first, attend):
                T = TB * (B + 1) + t
                for k in range(XT):
                    X = NX * B + XT * t + k
                    if not (first and k == 0):
                        hidden_hi(X - 1, (k - 1) % RING)
                    hidden(X, k)
                    if not attend:
                        continue
                    if k == 0:
                        if not first:
                            logits_exp(T - 1)
                        normed_t(T, 0)
                    if k == 1:
                        q_part(T)
                    if k == 2:
                        if not first:
                            combine_t(T - 1)
                        exps(T)
                    if k == 4:
                        prob_t(T)
                    if k == 5:
                        heads(T)
                    if k == 7:
                        normed_t(T, 1)
                    if k == 8:
                        logits_t(T)

            with act.Fori(0, TB) as t:
                normed_t(t, 0)
                q_part(t)
                exps(t)
                prob_t(t)
                heads(t)
                normed_t(t, 1)
                logits_t(t)
                logits_exp(t)
                combine_t(t)

            def moe_block(B, attend):
                tile_step(B, 0, True, attend)
                with act.Fori(1, TB) as t:
                    tile_step(B, t, False, attend)
                hidden_hi(NX * B + NX - 1, (NX - 1) % RING)
                if attend:
                    T = TB * (B + 1) + TB - 1
                    logits_exp(T)
                act.wait_ge(s_dn, NX * B + NX + 3)
                for c in range(KC):
                    nc.scalar.activation(y_t[:, c, :], acc[:, c, :], ACT.Copy, scale=tanh_g[:, 1:2]).then_inc(s_y, 1)
                if attend:
                    combine_t(T)

            with act.Fori(0, N_BLK - 1) as B:
                moe_block(B, True)
            moe_block(N_BLK - 1, False)

        @block.vector
        def _(dve):
            V = nc.vector
            V.memset(raw_a[:, INNER:2 * INNER], 0.0)
            V.memset(raw_b[:, INNER:2 * INNER], 0.0)
            V.memset(ctx_raw[:], 0.0)
            V.memset(mask_u8[:], 1)
            V.memset(prob[:, HJ:NCH * P], 0.0)
            V.memset(k_hi[:].bitcast(F32), 0.0)
            V.memset(k_lo[:].bitcast(F32), 0.0)
            V.memset(gate_hi[:].bitcast(F32), 0.0)
            V.memset(gate_lo[:].bitcast(F32), 0.0)
            V.memset(win_hi[:].bitcast(F32), 0.0)
            V.memset(win_lo[:].bitcast(F32), 0.0)
            V.memset(comb[:], 0.0)
            V.memset(row0[:], 0.0)
            dve.drain()
            V.memset(row0[0:1, :], 1.0)
            V.memset(ones_row[:], 1.0).then_inc(s_ones, 1)
            dve.drain()
            V.memset(nmax[:], 0.0).then_inc(s_zero, 1)
            dve.sem_inc(s_g, 3)
            dve.sem_inc(s_x1, 1)
            dve.sem_inc(s_kvl, 6)
            dve.sem_inc(s_out, 2)

            def split(dst_hi, dst_lo, raw):
                V.tensor_copy(dst_hi, raw)
                dve.drain()
                return V.tensor_tensor(dst_lo, raw, dst_hi.bitcast(F32), ALU.subtract)

            dve.wait_ge(s_const, 16 * 8)
            V.tensor_scalar(mask_add[:], mask_u8[:], -1.0, BIG, ALU.add, ALU.mult).then_inc(s_mask, 1)
            split(gate_hi[:, :, 0:NE], gate_lo[:, :, 0:NE], gate_raw[:])
            dve.wait_ge(s_wa, 16 * 7)
            split(wk_hi, wk_lo, raw_a[:, 0:2 * INNER]).then_inc(s_split, 1)
            split(wv_hi, wv_lo, raw_b[:, 0:2 * INNER])
            split(wq_hi[:], wq_lo[:], raw_c[:, 0:KC * INNER])
            with dve.Fori(0, NB) as b:
                dve.wait_ge(s_kvp, 2 * b + 2)
                split(win_hi[:, :, P:P + J], win_lo[:, :, P:P + J],
                      ctx_raw[:, bass.ds(b, 1), :, :].rearrange("p a c j -> p (a c) j")).then_inc(s_win, 1)
                for m in range(MC):
                    src = ps[:, m // 3, (m % 3) * J:(m % 3 + 1) * J]
                    if m == 0:
                        dve.wait_ge(s_kvh, 6 * b + 1)
                    if m == 3:
                        dve.wait_ge(s_kvh, 6 * b + 2)
                    V.tensor_tensor(k_lo[0:64, 2 * m, :], src[0:64, :], k_hi[0:64, 2 * m, :].bitcast(F32), ALU.subtract)
                    i = V.tensor_tensor(k_lo[64:P, 2 * m + 1, :], src[64:P, :], k_hi[64:P, 2 * m + 1, :].bitcast(F32), ALU.subtract)
                    if m >= 2:
                        i.then_inc(s_kvl, 1)
                for j in range(4):
                    n = min(4, NAV - 4 * j) * P
                    dve.wait_ge(s_kvh, 6 * b + 3 + j)
                    V.tensor_tensor(v_lo[:, 512 * j:512 * j + n], ps[:, 2 + j, 0:n],
                                    v_hi[:, 512 * j:512 * j + n].bitcast(F32), ALU.subtract).then_inc(s_kvl, 1)
                dve.wait_ge(s_kvs, 64 * b + 64)
            dve.wait_ge(s_wa, 16 * 8)
            split(wo_hi[:], wo_lo[:], raw_a[:, 0:MC * D]).then_inc(s_split, 1)

            def norm(T, ln, src):
                st, mv = ln_s[:, 0:6], ln_s[:, 6:8]
                ve, y, a = ln_s[:, 8:9], ln_s[:, 9:10], ln_s[:, 10:11]
                V.bn_stats(st, src)
                dve.drain()
                V.bn_aggr(mv, st)
                dve.drain()
                V.tensor_scalar(ve, mv[:, 1:2], EPS, None, ALU.add)
                dve.drain()
                V.tensor_scalar(ln_i[:, 0:1], ve.bitcast(I32), 1, None, ALU.logical_shift_right)
                dve.drain()
                V.tensor_scalar(y.bitcast(I32), ln_i[:, 0:1], -1.0, RSQRT_MAGIC, ALU.mult, ALU.add)
                dve.drain()
                for _ in range(4):
                    V.scalar_tensor_tensor(a, y, ve, y, ALU.mult, ALU.mult)
                    dve.drain()
                    V.tensor_scalar(a, a, -0.5, 1.5, ALU.mult, ALU.add)
                    dve.drain()
                    V.tensor_tensor(y, y, a, ALU.mult)
                    dve.drain()
                V.tensor_scalar(x_n[:], src, mv[:, 0:1], y, ALU.subtract, ALU.mult).then_inc(s_xn, 1)

            def norm_in(T):
                dve.wait_ge(s_x, 16 * T + 16)
                norm(T, 0, x_in[:])

            def normed_t(T, ln):
                dve.wait_ge(s_xth, 2 * T + ln + 1)
                if ln == 0:
                    V.tensor_tensor(x1t_lo[:], att[:, 0, 0:EW], x1t_hi[:].bitcast(F32), ALU.subtract).then_inc(s_xtl, 1)
                else:
                    par, col = T // TB % 2, T % TB * P
                    hi = x2t_hi[:, bass.ds(par, 1), :, bass.ds(col, P)].rearrange("p a c n -> p (a c) n")
                    lo = x2t_lo[:, bass.ds(par, 1), :, bass.ds(col, P)].rearrange("p a c n -> p (a c) n")
                    V.tensor_tensor(lo, att[:, 2, 0:EW].rearrange("p (c n) -> p c n", c=KC), hi.bitcast(F32),
                                    ALU.subtract).then_inc(s_xtl, 1)

            def q_part(T):
                dve.wait_ge(s_qh, T + 1)
                V.tensor_tensor(q_lo[:], att[:, 1, :], q_hi[:].bitcast(F32), ALU.subtract).then_inc(s_ql, 1)

            def maxima(T):
                h = 0
                for bank, nh in enumerate(BANK_H):
                    dve.wait_ge(s_s, 3 * T + bank + 1)
                    V.tensor_reduce(rsum[:, h:h + nh], att[:, bank, 0:nh * J].rearrange("p (a j) -> p a j", a=nh),
                                    op=ALU.max, axis=AX_X)
                    dve.drain()
                    V.tensor_scalar(nmax[:, h:h + nh], rsum[:, h:h + nh], -SCALE, None, ALU.mult).then_inc(s_nm, 1)
                    h += nh

            def normalise(T):
                dve.wait_ge(s_p, 3 * T + 3)
                V.reciprocal(rsum[:], psum_exp[:])
                dve.drain()
                p3 = prob[:, 0:HJ].rearrange("p (h j) -> p h j", h=NH)
                V.tensor_tensor(p3, p3, rsum[:].unsqueeze(2).broadcast_to([P, NH, J]), ALU.mult).then_inc(s_pn, 1)

            def prob_t(T):
                for bank in range(3):
                    n = min(4, NCH - 4 * bank) * P
                    dve.wait_ge(s_pth, 3 * T + bank + 1)
                    V.tensor_tensor(pt_lo[:, 512 * bank:512 * bank + n], att[:, bank, 0:n],
                                    pt_hi[:, 512 * bank:512 * bank + n].bitcast(F32), ALU.subtract).then_inc(s_ptl, 1)

            def heads(T):
                dve.wait_ge(s_ah, T + 1)
                V.tensor_tensor(at_lo[:], att[:, 0, :], at_hi[:].bitcast(F32), ALU.subtract).then_inc(s_al, 1)

            def residual(T, blk):
                dst = x1[:, bass.ds(T // TB % 2, 1), bass.ds(T % TB, 1), :].rearrange("p a t d -> p (a t d)")
                dve.wait_ge(s_o, T + 1)
                dve.wait_ge(s_x1free, blk if blk is not None else 1)
                V.tensor_tensor(x_n[:], att[:, 1, 0:D], bias_o[:], ALU.add)
                dve.drain()
                V.scalar_tensor_tensor(dst, x_n[:], tanh_g[:, 0:1], x_in[:], ALU.mult, ALU.add).then_inc(s_x1, 1)
                dve.drain()
                norm(T, 1, dst)

            def router(T):
                dve.wait_ge(s_e, T + 1)
                V.tensor_scalar(score[:], exp_l[:], 1.0, None, ALU.add)
                dve.drain()
                V.reciprocal(score[:], score[:])
                dve.drain()
                V.tensor_tensor(biased[:], score[:], bias_e[:], ALU.add)
                dve.drain()
                mx, mn = grp[:, 0:16], grp[:, 16:32]
                V.tensor_tensor(mx, biased[:, 0:NE:2], biased[:, 1:NE:2], ALU.max)
                V.tensor_tensor(mn, biased[:, 0:NE:2], biased[:, 1:NE:2], ALU.min)
                dve.drain()
                first, other, low = grp[:, 32:40], grp[:, 40:48], grp[:, 48:56]
                V.tensor_tensor(first, mx[:, 0:16:2], mx[:, 1:16:2], ALU.max)
                V.tensor_tensor(other, mx[:, 0:16:2], mx[:, 1:16:2], ALU.min)
                V.tensor_tensor(low, mn[:, 0:16:2], mn[:, 1:16:2], ALU.max)
                dve.drain()
                V.tensor_tensor(other, other, low, ALU.max)
                dve.drain()
                V.tensor_tensor(first, first, other, ALU.add)
                dve.drain()
                best, idx_g = grp[:, 56:64], grp[:, 64:72]
                V.max(best, first)
                dve.drain()
                V.max_index(grp_i[:, 0:8], best, first)
                dve.drain()
                V.tensor_copy(idx_g, grp_i[:, 0:8])
                dve.drain()
                V.tensor_tensor(hot_g[:], iota_f[:, 0:NG].unsqueeze(1).broadcast_to([P, TOPG, NG]),
                                idx_g[:, 0:TOPG].unsqueeze(2).broadcast_to([P, TOPG, NG]), ALU.is_equal)
                dve.drain()
                V.tensor_reduce(low, hot_g[:].rearrange("p k g -> p g k"), op=ALU.max, axis=AX_X)
                dve.drain()
                V.tensor_tensor(masked[:].rearrange("p (g e) -> p g e", g=NG), biased[:].rearrange("p (g e) -> p g e", g=NG),
                                low.unsqueeze(2).broadcast_to([P, NG, GE]), ALU.mult)
                dve.drain()
                V.tensor_scalar(masked[:], masked[:], 0.0, None, ALU.add)
                dve.drain()
                V.max(best, masked[:])
                dve.drain()
                V.max_index(grp_i[:, 8:16], best, masked[:])
                dve.drain()
                V.tensor_copy(idx_g, grp_i[:, 8:16])
                dve.drain()
                V.tensor_tensor(hot[:], iota_f[:].unsqueeze(1).broadcast_to([P, TOPK, NE]),
                                idx_g[:, 0:TOPK].unsqueeze(2).broadcast_to([P, TOPK, NE]), ALU.is_equal)
                dve.drain()
                V.tensor_reduce(sel[:], hot[:].rearrange("p k e -> p e k"), op=ALU.max, axis=AX_X)
                dve.drain()
                total = grp[:, 72:73]
                V.tensor_tensor_reduce(out=weighted[:], in0=sel[:], in1=score[:], scale=1.0, scalar=0.0,
                                       op0=ALU.mult, op1=ALU.add, accum_out=total)
                dve.drain()
                V.tensor_scalar(total, total, 1e-20, None, ALU.add)
                dve.drain()
                V.reciprocal(total, total)
                dve.drain()
                V.tensor_scalar(comb[:, 0:NE], weighted[:], total, ROUTED_SCALE, ALU.mult, ALU.mult).then_inc(s_c, 1)

            def hidden_lo(X, k):
                r = k % RING
                dve.wait_ge(s_gh, X + 1)
                V.tensor_tensor(act_lo[:, r, :], act_f[:, r, :], act_hi[:, r, :].bitcast(F32), ALU.subtract).then_inc(s_gl, 1)

            def hidden(X, B, t, k):
                r = k % RING
                dve.wait_ge(s_sq, X + 1)
                dve.wait_ge(s_cb[r], 16 * ((NX // RING) * B + (XT // RING) * t + k // RING + 1))
                V.tensor_tensor(act_f[:, r, :], act_f[:, r, :], comb_b[:, r, :], ALU.mult).then_inc(s_g, 1)

            def tile_step(B, t, first, attend):
                T = TB * (B + 1) + t
                for k in range(XT):
                    X = NX * B + XT * t + k
                    if not (first and k == 0):
                        hidden_lo(X - 1, (k - 1) % RING)
                    hidden(X, B, t, k)
                    if not attend:
                        continue
                    if k == 0:
                        if not first:
                            router(T - 1)
                        norm_in(T)
                        normed_t(T, 0)
                    if k == 1:
                        q_part(T)
                    if k == 2:
                        maxima(T)
                    if k == 3:
                        normalise(T)
                    if k == 4:
                        prob_t(T)
                    if k == 5:
                        heads(T)
                    if k == 6:
                        residual(T, B + 1)
                    if k == 7:
                        normed_t(T, 1)

            dve.wait_ge(s_tanh, 1)
            with dve.Fori(0, TB) as t:
                norm_in(t)
                normed_t(t, 0)
                q_part(t)
                maxima(t)
                normalise(t)
                prob_t(t)
                heads(t)
                residual(t, None)
                normed_t(t, 1)
                router(t)

            def moe_block(B, attend):
                tile_step(B, 0, True, attend)
                with dve.Fori(1, TB) as t:
                    tile_step(B, t, False, attend)
                hidden_lo(NX * B + NX - 1, (NX - 1) % RING)
                if attend:
                    router(TB * (B + 1) + TB - 1)
                for j in range(2):
                    dst = x1[:, bass.ds(B % 2, 1), 2 * j:2 * j + 2, :].rearrange("p a t d -> p (a t d)")
                    dve.wait_ge(s_yt, 2 * B + j + 1)
                    V.tensor_tensor(dst, acc[:, j, :], dst, ALU.add).then_inc(s_out, 1)

            with dve.Fori(0, N_BLK - 1) as B:
                moe_block(B, True)
            moe_block(N_BLK - 1, False)

        @block.tensor
        def _(pe):
            pe.sem_inc(s_up, 3)
            pe.sem_inc(s_dn, 3)
            pe.sem_inc(s_kvp, 2)
            pe.wait_ge(s_split, 1)
            with pe.Fori(0, NB) as b:
                pe.wait_ge(s_win, b + 1)
                pe.wait_ge(s_kvl, 6 * b + 6)
                for m in range(MC):
                    o = ps[:, m // 3, (m % 3) * J:(m % 3 + 1) * J]
                    for c in range(2):
                        w = slice(c * INNER + m * P, c * INNER + (m + 1) * P)
                        ins = three(o, wk_hi[:, w], wk_lo[:, w], win_hi[:, c, P:P + J], win_lo[:, c, P:P + J], c == 0, c == 1)
                ins.then_inc(s_kvp, 1)
                for n, (m, ch) in enumerate(AV):
                    for i in range(2):
                        h = 2 * m + i
                        at = P + min(max(ch * P - h * J, -P), J)
                        o = ps[:, 2 + n // 4, n % 4 * P + i * DH:n % 4 * P + (i + 1) * DH]
                        for c in range(2):
                            w = slice(c * INNER + h * DH, c * INNER + (h + 1) * DH)
                            ins = three(o, win_hi[:, c, at:at + P], win_lo[:, c, at:at + P], wv_hi[:, w], wv_lo[:, w], c == 0, c == 1)
                ins.then_inc(s_kvp, 1)
            pe.wait_ge(s_kvl, 6 * NB + 6)
            pe.wait_ge(s_split, 2)
            pe.wait_ge(s_mask, 1)

            def normed_t(T, ln):
                pe.wait_ge(s_xn, 2 * T + ln + 1)
                for c in range(KC):
                    ins = nc.tensor.transpose(att[:, 2 * ln, c * P:(c + 1) * P], x_n[:, c * P:(c + 1) * P], ident[:])
                ins.then_inc(s_xt, 1)

            def q_part(T):
                pe.wait_ge(s_xtl, 2 * T + 1)
                for m in range(MC):
                    for c in range(KC):
                        w = slice(c * INNER + m * P, c * INNER + (m + 1) * P)
                        f = slice(c * P, (c + 1) * P)
                        ins = three(att[:, 1, m * P:(m + 1) * P], wq_hi[:, w], wq_lo[:, w], x1t_hi[:, f], x1t_lo[:, f], c == 0, c == KC - 1)
                ins.then_inc(s_q, 1)

            def scores(T, b):
                pe.wait_ge(s_ql, T + 1)
                pe.wait_ge(s_cts, T + 1)
                h = 0
                for bank, nh in enumerate(BANK_H):
                    for i in range(nh):
                        o = att[:, bank, i * J:(i + 1) * J]
                        f = slice(h // 2 * P, (h // 2 + 1) * P)
                        nc.tensor.matmul(o, row0[:], mask_add[:, bass.ds(b, 1), :].rearrange("p a j -> p (a j)"),
                                         start=True, stop=False, skip_group_check=True)
                        ins = three(o, q_hi[:, f], q_lo[:, f], k_hi[:, h, :], k_lo[:, h, :], False, True)
                        h += 1
                    ins.then_inc(s_s, 1)

            def prob_t(T):
                pe.wait_ge(s_pn, T + 1)
                for c in range(NCH):
                    ins = nc.tensor.transpose(att[:, c // 4, c % 4 * P:(c % 4 + 1) * P], prob[:, c * P:(c + 1) * P], ident[:])
                    if c % 4 == 3 or c == NCH - 1:
                        ins.then_inc(s_pt, 1)

            def heads(T):
                pe.wait_ge(s_ptl, 3 * T + 3)
                for n, (m, c) in enumerate(AV):
                    f, r = slice(n * P, (n + 1) * P), slice(c * P, (c + 1) * P)
                    ins = three(att[:, 0, m * P:(m + 1) * P], v_hi[:, f], v_lo[:, f], pt_hi[:, r], pt_lo[:, r],
                                n == 0 or AV[n - 1][0] != m, n == NAV - 1 or AV[n + 1][0] != m)
                ins.then_inc(s_a, 1)

            def attn_out(T):
                pe.wait_ge(s_al, T + 1)
                for m in range(MC):
                    f, w = slice(m * P, (m + 1) * P), slice(m * D, (m + 1) * D)
                    ins = three(att[:, 1, 0:D], at_hi[:, f], at_lo[:, f], wo_hi[:, w], wo_lo[:, w], m == 0, m == MC - 1)
                ins.then_inc(s_o, 1)

            def logits_t(T):
                pe.wait_ge(s_xtl, 2 * T + 2)
                par, col = T // TB % 2, T % TB * P
                for c in range(KC):
                    hi = x2t_hi[:, bass.ds(par, 1), c, bass.ds(col, P)].rearrange("p a n -> p (a n)")
                    lo = x2t_lo[:, bass.ds(par, 1), c, bass.ds(col, P)].rearrange("p a n -> p (a n)")
                    ins = three(att[:, 1, 256:384], gate_hi[:, c, :], gate_lo[:, c, :], hi, lo, c == 0, c == KC - 1)
                ins.then_inc(s_lt, 1)

            def logits(T):
                pe.wait_ge(s_lts, T + 1)
                nc.tensor.transpose(att[:, 1, 384:512], lt_sb[:], ident[:]).then_inc(s_l, 1)

            def combine_t(T):
                pe.wait_ge(s_c, T + 1)
                nc.tensor.transpose(att[:, 2, 256:384], comb[:], ident[:]).then_inc(s_ct, 1)

            def up(X, B, k):
                r = k % RING
                pe.wait_ge(s_wu, X + 1)
                for c in range(KC):
                    w = slice(c * P, (c + 1) * P)
                    hi = x2t_hi[:, bass.ds(B % 2, 1), c, :].rearrange("p a n -> p (a n)")
                    lo = x2t_lo[:, bass.ds(B % 2, 1), c, :].rearrange("p a n -> p (a n)")
                    ins = three(hid[:, r, :], wu_hi[:, r, w], wu_lo[:, r, w], hi, lo, c == 0, c == KC - 1)
                ins.then_inc(s_up, 1)

            def down(X, k, start, stop):
                r = k % RING
                pe.wait_ge(s_wd, X + 1)
                pe.wait_ge(s_gl, X + 1)
                for c in range(KC):
                    w = slice(c * P, (c + 1) * P)
                    ins = three(acc[:, c, :], wd_hi[:, r, w], wd_lo[:, r, w], act_hi[:, r, :], act_lo[:, r, :], start, stop)
                ins.then_inc(s_dn, 1)

            def tile_step(B, t, first, attend):
                T = TB * (B + 1) + t
                for k in range(XT):
                    X = NX * B + XT * t + k
                    up(X, B, k)
                    if first and k == 2:
                        pe.wait_ge(s_out, 2 * B + 2)
                    if not first or k >= 2:
                        down(X - 2, (k - 2) % RING, first and k == 2, False)
                    if not attend:
                        continue
                    if k == 0:
                        if not first:
                            logits(T - 1)
                        normed_t(T, 0)
                    if k == 1:
                        if not first:
                            pe.wait_ge(s_e, T)
                        q_part(T)
                    if k == 2:
                        if not first:
                            combine_t(T - 1)
                        scores(T, (B + 1) // BLK_B)
                    if k == 4:
                        prob_t(T)
                    if k == 5:
                        heads(T)
                    if k == 6:
                        attn_out(T)
                    if k == 7:
                        normed_t(T, 1)
                    if k == 8:
                        logits_t(T)

            pe.wait_ge(s_kv, 64)
            with pe.Fori(0, TB) as t:
                normed_t(t, 0)
                q_part(t)
                scores(t, 0)
                prob_t(t)
                heads(t)
                attn_out(t)
                normed_t(t, 1)
                logits_t(t)
                logits(t)
                combine_t(t)

            def moe_block(B, attend):
                pe.wait_ge(s_xtl, 2 * TB * B + 2 * TB)
                if attend:
                    pe.wait_ge(s_kv, 64 * B + 128)
                tile_step(B, 0, True, attend)
                with pe.Fori(1, TB) as t:
                    tile_step(B, t, False, attend)
                for e in (NX - 2, NX - 1):
                    down(NX * B + e, e, False, e == NX - 1)
                if attend:
                    T = TB * (B + 1) + TB - 1
                    logits(T)
                pe.wait_ge(s_y, 2 * B + 2)
                for i in range(TB):
                    for c in range(KC):
                        ins = nc.tensor.transpose(acc[:, i // 2, i % 2 * D + c * P:i % 2 * D + (c + 1) * P],
                                                  y_t[:, c, i * P:(i + 1) * P], ident[:])
                    if i % 2:
                        ins.then_inc(s_yt, 1)
                if attend:
                    combine_t(TB * (B + 1) + TB - 1)

            with pe.Fori(0, N_BLK - 1) as B:
                moe_block(B, True)
            moe_block(N_BLK - 1, False)


_INS = ["x", "ctx_t", "mask", "g_xattn", "g_ffn", "w_q", "w_k", "w_v", "w_o", "b_o", "gate_t", "e_bias",
        "w_moe", "eye", "iota"]


def kernel(x, ctx_768, mask_BxS2_bk0, g_xattn, g_ffn, L0_xattn_W_q, L0_xattn_W_k, L0_xattn_W_v, L0_xattn_W_o,
           L0_xattn_b_o, L0_ffn_gate_w, L0_ffn_e_bias, L0_ffn_up_w, L0_ffn_down_w, L0_ffn_shared_up_w,
           L0_ffn_shared_down_w):
    import numpy as np
    import concourse.bacc as bacc
    from concourse.bass_utils import run_bass_kernel_spmd

    x = np.asarray(x)
    shape = x.shape
    d = shape[-1]
    up, down = np.asarray(L0_ffn_up_w), np.asarray(L0_ffn_down_w)
    part = up.shape[1]
    sup = np.asarray(L0_ffn_shared_up_w).reshape(-1, part, d)
    sdn = np.asarray(L0_ffn_shared_down_w).reshape(d, -1, part).transpose(1, 0, 2)
    ups = np.concatenate([up, sup])
    downs = np.concatenate([down, sdn])
    ups = ups.transpose(2, 0, 1).reshape(d // P, P, -1, part).transpose(1, 2, 0, 3).reshape(P, -1, d)
    downs = downs.transpose(2, 0, 1)
    arrays = {
        "x": x.reshape(-1, d),
        "ctx_t": np.asarray(ctx_768).transpose(0, 2, 1),
        "mask": np.asarray(mask_BxS2_bk0),
        "g_xattn": np.asarray(g_xattn), "g_ffn": np.asarray(g_ffn),
        "w_q": np.asarray(L0_xattn_W_q), "w_k": np.asarray(L0_xattn_W_k), "w_v": np.asarray(L0_xattn_W_v),
        "w_o": np.asarray(L0_xattn_W_o), "b_o": np.asarray(L0_xattn_b_o),
        "gate_t": np.asarray(L0_ffn_gate_w).T, "e_bias": np.asarray(L0_ffn_e_bias),
        "w_moe": np.concatenate([ups, downs], axis=2),
        "eye": np.eye(P, dtype=np.float32),
        "iota": np.tile(np.arange(len(L0_ffn_gate_w), dtype=np.float32), (P, 1)),
    }
    nc = bacc.Bacc("TRN2", target_bir_lowering=False, num_devices=1)
    feeds, args = {}, []
    for name in _INS:
        a = np.ascontiguousarray(arrays[name])
        feeds[f"in_{name}"] = a
        args.append(nc.dram_tensor(f"in_{name}", a.shape, mybir.dt.from_np(a.dtype), kind="ExternalInput").ap())
    out = nc.dram_tensor("out", arrays["x"].shape, F32, kind="ExternalOutput").ap()
    flamingo_block(nc, *args, out)
    r = run_bass_kernel_spmd(nc, [feeds], core_ids=[0])
    return r.results[0]["out"].reshape(shape)
```

```python
from contextlib import ExitStack

import concourse.bass as bass
from concourse import mybir

F32 = mybir.dt.float32
F32R = mybir.dt.float32r
BF16 = mybir.dt.bfloat16
I32 = mybir.dt.int32
U32 = mybir.dt.uint32
U8 = mybir.dt.uint8
ALU = mybir.AluOpType
ACT = mybir.ActivationFunctionType
AX_X = mybir.AxisListType.X

P = 128
EPS = 1e-5
BIG = 3.0e38
RSQRT_MAGIC = 1597463007.0
ROUTED_SCALE = 2.5


def flamingo_block(nc, x, ctx_t, mask, g_xattn, g_ffn, w_q, w_k, w_v, w_o, b_o, gate_t, e_bias,
                   w_moe, eye, iota, out):
    n_tok, D = x.shape
    NB, CD, J = ctx_t.shape
    INNER = w_q.shape[1]
    DH = 64
    NH = INNER // DH
    SCALE = float(DH) ** -0.5
    KC = D // P
    MC = INNER // P
    NE = e_bias.shape[0]
    NG, GE, TOPG, TOPK = 8, NE // 8, 4, 6
    NX = w_moe.shape[1]
    NS = NX - NE
    EW = KC * P
    BT = 512
    TB = BT // P
    N_BLK = n_tok // BT
    XT = NX // TB
    BLK_B = n_tok // NB // BT
    BANK_H = (3, 3, 2)
    HJ = NH * J
    NCH = -(-HJ // P)
    SCORES = ((0, 0, (0, 1)), (0, 2 * J, (2,)), (1, 0, (3,)), (1, J, (4, 5)), (2, 0, (6, 7)))
    AV = [(m, c) for m in range(MC) for c in range(NCH)
          if c * P < (2 * m + 2) * J and (c + 1) * P > 2 * m * J]
    NAV = len(AV)
    KV_K, KV_V = NH * J, NAV * P
    KV = 2 * KV_K + 2 * KV_V
    WIN = P + J + P
    RING = 3
    assert XT % RING == 0 and NX == TB * XT and (NB - 1) * KV <= NX * 2 * EW

    x_tiles = x.rearrange("(t p) d -> t p d", p=P)
    out_blk = out.rearrange("(b t p) d -> b p t d", p=P, t=TB)
    comb_dram = nc.dram_tensor("combine_weights", [NX, n_tok], F32, kind="Internal").ap()
    kv_dram = nc.dram_tensor("keys_values", [NB - 1, P, KV], F32, kind="Internal").ap()

    with ExitStack() as ctx:
        def sb(name, shape, dt):
            return ctx.enter_context(nc.sbuf_tensor(name, shape, dt))

        def sem(name):
            return ctx.enter_context(nc.semaphore(name))

        ps = ctx.enter_context(nc.psum_tensor("ps", [P, 8, 512], F32))
        acc = ps[:, 0:2, :]
        hid = ps[:, 2:5, :]
        att = ps[:, 5:8, :]

        w_raw = sb("w_raw", [P, NX, 2 * EW], F32)
        wu_hi = sb("wu_hi", [P, RING, EW], F32R)
        wu_lo = sb("wu_lo", [P, RING, EW], F32R)
        wd_hi = sb("wd_hi", [P, RING, EW], F32R)
        wd_lo = sb("wd_lo", [P, RING, EW], F32R)
        wq_hi = sb("wq_hi", [P, KC * INNER], F32R)
        wq_lo = sb("wq_lo", [P, KC * INNER], F32R)
        wo_hi = sb("wo_hi", [P, MC * D], F32R)
        wo_lo = sb("wo_lo", [P, MC * D], F32R)
        kv = sb("kv", [P, KV], F32R)

        def kv_parts(at):
            k = [at(i * KV_K, KV_K).rearrange("p (h j) -> p h j", h=NH) for i in range(2)]
            return k + [at(2 * KV_K + i * KV_V, KV_V) for i in range(2)]

        k_hi, k_lo, v_hi, v_lo = kv_parts(lambda c, n: kv[:, c:c + n])
        ident = sb("ident", [P, P], F32)
        iota_f = sb("iota_f", [P, NE], F32)
        bias_e = sb("bias_e", [P, NE], F32)
        bias_o = sb("bias_o", [P, D], F32)
        gates = sb("gates", [P, 2], F32)
        tanh_g = sb("tanh_g", [P, 2], F32)
        mask_u8 = sb("mask_u8", [P, NB, J], U8)
        mask_add = sb("mask_add", [P, NB, J], BF16)
        row0 = sb("row0", [P, P], BF16)
        ones = sb("ones", [P, 1], F32)
        y_t = sb("y_t", [P, KC, BT], F32)
        ones_row = y_t[0:NS, 1, :]
        gate_w = sb("gate_w", [P, KC, NE], F32)
        x_in = sb("x_in", [P, 2, D], F32)
        x_n1 = sb("x_n1", [P, D], F32)
        x_n2 = y_t[:, 0, 0:D]
        x1t_hi = sb("x1t_hi", [P, EW], F32R)
        x1t_lo = sb("x1t_lo", [P, EW], F32R)
        q_hi = sb("q_hi", [P, INNER], F32R)
        q_lo = sb("q_lo", [P, INNER], F32R)
        prob = sb("prob", [P, NCH * P], F32)
        pt_hi = sb("pt_hi", [P, NCH * P], F32R)
        pt_lo = sb("pt_lo", [P, NCH * P], F32R)
        at_hi, at_lo = q_hi, q_lo
        nmax = sb("nmax", [P, NH], F32)
        psum_exp = sb("psum_exp", [P, NH], F32)
        rsum = sb("rsum", [P, NH], F32)
        ln_s = sb("ln_s", [P, 16], F32)
        ln_i = sb("ln_i", [P, 2], I32)
        x1 = sb("x1", [P, 2, TB, D], F32)
        x2t_hi = sb("x2t_hi", [P, 2, KC, BT], F32R)
        x2t_lo = sb("x2t_lo", [P, 2, KC, BT], F32R)
        x2t_f = sb("x2t_f", [P, EW], F32)
        exp_l = sb("exp_l", [P, NE], F32)
        score = sb("score", [P, NE], F32)
        biased = sb("biased", [P, NE], F32)
        grp = sb("grp", [P, 96], F32)
        grp_i = sb("grp_i", [P, 16], U32)
        hot_g = sb("hot_g", [P, TOPG, NG], F32)
        masked = sb("masked", [P, NE], F32)
        hot = sb("hot", [P, TOPK, NE], F32)
        sel = sb("sel", [P, NE], F32)
        weighted = sb("weighted", [P, NE], F32)
        comb = sb("comb", [P, P], F32)
        comb_t = sb("comb_t", [NE, P], F32)
        comb_b = sb("comb_b", [P, RING, BT], F32)
        act_f = sb("act_f", [P, RING, BT], F32)
        act_hi = sb("act_hi", [P, RING, BT], F32R)
        act_lo = sb("act_lo", [P, RING, BT], F32R)

        w_cols = w_raw[:, :, :].rearrange("p e n -> p (e n)")
        w_cols_r = w_cols.bitcast(F32R)
        raw_a = act_f[:, :, :].rearrange("p a b -> p (a b)")
        raw_b = comb_b[:, :, :].rearrange("p a b -> p (a b)")
        raw_c = x1[:, :, :, :].rearrange("p a t d -> p (a t d)")
        ctx_raw = prob[:, 0:NB * 2 * J].rearrange("p (b c j) -> p b c j", b=NB, c=2)
        wk_hi = act_hi[:, :, :].rearrange("p a b -> p (a b)")[:, 0:2 * INNER]
        wk_lo = act_lo[:, :, :].rearrange("p a b -> p (a b)")[:, 0:2 * INNER]
        wv_hi = x2t_hi[:, 1, :, :].rearrange("p a b -> p (a b)")
        wv_lo = x2t_lo[:, 1, :, :].rearrange("p a b -> p (a b)")
        win_hi = x2t_hi[:, 0, :, :].rearrange("p a b -> p (a b)")[:, 0:2 * WIN].rearrange("p (c w) -> p c w", c=2)
        win_lo = x2t_lo[:, 0, :, :].rearrange("p a b -> p (a b)")[:, 0:2 * WIN].rearrange("p (c w) -> p c w", c=2)

        s_zero = sem("rows_cleared")
        s_kz = sem("key_rows_cleared")
        s_const = sem("constants_loaded")
        s_wa = sem("attention_weights_loaded")
        s_wm = sem("expert_weights_loaded")
        s_ones = sem("ones_ready")
        s_mask = sem("mask_ready")
        s_tanh = sem("tanh_ready")
        s_split = sem("attention_weights_split")
        s_win = sem("context_split")
        s_kvp = sem("keys_values_in_psum")
        s_kvh = sem("keys_values_hi")
        s_kvl = sem("keys_values_lo")
        s_kvs = sem("keys_values_stored")
        s_x = sem("x_loaded")
        s_k = sem("keys_loaded")
        s_v = sem("values_loaded")
        s_xn = [sem(f"normed_{i}") for i in (1, 2)]
        s_xt = [sem(f"normed_{i}_t_psum") for i in (1, 2)]
        s_xth = sem("normed_1_t_hi")
        s_xtl = [sem(f"normed_{i}_t_lo") for i in (1, 2)]
        s_q = sem("q_psum")
        s_qh = sem("q_hi_ready")
        s_ql = sem("q_lo_ready")
        s_s = sem("scores_psum")
        s_nm = sem("max_ready")
        s_p = sem("exp_ready")
        s_pn = sem("prob_ready")
        s_pt = sem("prob_t_psum")
        s_pth = sem("prob_t_hi")
        s_ptl = sem("prob_t_lo")
        s_a = sem("heads_psum")
        s_ah = sem("heads_hi")
        s_al = sem("heads_lo")
        s_o = sem("attn_out_psum")
        s_x1 = sem("residual_ready")
        s_x2f = sem("normed_2_t_hi_and_copy")
        s_l = sem("logits_psum")
        s_e = sem("logits_exp")
        s_c = sem("combine_ready")
        s_ct = sem("combine_t_psum")
        s_cts = sem("combine_t_sbuf")
        s_cd = sem("combine_stored")
        s_wu = sem("up_staged")
        s_wd = sem("down_staged")
        s_cb = [sem(f"combine_row_{i}") for i in range(RING)]
        s_up = sem("hidden_psum")
        s_sq = sem("squared")
        s_g = sem("weighted_hidden")
        s_gh = sem("hidden_hi")
        s_gl = sem("hidden_lo")
        s_dn = sem("down_done")
        s_y = sem("sum_t_sbuf")
        s_yt = sem("sum_psum")
        s_out = sem("output_ready")
        s_st = sem("output_stored")
        s_x1free = sem("residual_free")

        block = ctx.enter_context(nc.Block())

        def three(o, l_hi, l_lo, r_hi, r_lo, start, stop):
            nc.tensor.matmul(o, l_hi, r_lo, start=start, stop=False, skip_group_check=True)
            nc.tensor.matmul(o, l_lo, r_hi, start=False, stop=False, skip_group_check=True)
            return nc.tensor.matmul(o, l_hi, r_hi, start=False, stop=stop, skip_group_check=True)


        @block.sync
        def _(sp):
            sp.sem_inc(s_x1free, 1)
            for dst, src in ((ident[:], eye), (iota_f[:], iota),
                             (bias_e[:], e_bias.partition_broadcast(P)),
                             (bias_o[:], b_o.partition_broadcast(P)),
                             (gates[:, 0:1], g_xattn.partition_broadcast(P)),
                             (gates[:, 1:2], g_ffn.partition_broadcast(P)),
                             (gate_w[:], gate_t.rearrange("(c p) e -> p c e", p=P))):
                sp.dma_start(dst, src).then_inc(s_const, 16)
            sp.wait_ge(s_zero, 1)
            sp.dma_start(mask_u8[0:1, :, :], mask.rearrange("(a b) j -> a b j", a=1)).then_inc(s_const, 16)
            half = CD - P
            for dst, src in (
                (raw_a[:, 0:INNER], w_k[0:P, :]), (raw_a[0:half, INNER:2 * INNER], w_k[P:CD, :]),
                (raw_b[:, 0:INNER], w_v[0:P, :]), (raw_b[0:half, INNER:2 * INNER], w_v[P:CD, :]),
                (ctx_raw[:, :, 0, :], ctx_t[:, 0:P, :].rearrange("b p j -> p b j")),
                (ctx_raw[0:half, :, 1, :], ctx_t[:, P:CD, :].rearrange("b p j -> p b j")),
                (raw_c[:, 0:KC * INNER].rearrange("p (c n) -> p c n", c=KC), w_q.rearrange("(c p) n -> p c n", p=P)),
            ):
                sp.dma_start(dst, src).then_inc(s_wa, 16)
            sp.wait_ge(s_split, 1)
            sp.dma_start(raw_a[:, 0:MC * D].rearrange("p (c n) -> p c n", c=MC),
                         w_o.rearrange("(c p) n -> p c n", p=P)).then_inc(s_wa, 16)
            sp.wait_ge(s_ones, 1)
            sp.dma_start(comb_dram[0:NS, :].rearrange("e (a n) -> e a n", n=512),
                         ones_row.unsqueeze(1).broadcast_to([NS, n_tok // 512, 512])).then_inc(s_cd, 16)

            def load_x(T):
                sp.wait_ge(s_x1, T + 1)
                sp.dma_start(x_in[:, bass.ds(T % 2, 1), :].rearrange("p a d -> p (a d)"), x_tiles[T]).then_inc(s_x, 16)

            load_x(0)
            for i in range(NB - 1):
                sp.wait_ge(s_kvl, 6 * i + 12)
                sp.dma_start(kv_dram[i], w_cols[:, i * KV:(i + 1) * KV]).then_inc(s_kvs, 16)
            sp.wait_ge(s_xn[0], 1)
            load_x(1)
            sp.wait_ge(s_kvs, 16 * (NB - 1))
            for e0 in range(0, NX, 12):
                sp.dma_start(w_raw[:, e0:e0 + 12, :], w_moe[:, e0:e0 + 12, :]).then_inc(s_wm, 16)

            def load_context(i):
                sp.dma_start(kv[:, 0:2 * KV_K].bitcast(F32), kv_dram[i][:, 0:2 * KV_K]).then_inc(s_k, 16)
                sp.dma_start(kv[:, 2 * KV_K:KV].bitcast(F32), kv_dram[i][:, 2 * KV_K:KV]).then_inc(s_v, 16)

            def store_combine(T):
                sp.wait_ge(s_cts, T + 2)
                sp.wait_ge(s_cd, 16 * T + 16)
                sp.dma_start(comb_dram[NS:NX, bass.ds(T * P, P)], comb_t[:]).then_inc(s_cd, 16)

            def load_row(B, t, k, first):
                X = NX * B + XT * t + k
                sp.wait_ge(s_g, X + 1)
                if first and k == NS:
                    sp.wait_ge(s_cd, 16 * (TB * B + TB) + 16)
                sp.dma_start(comb_b[:, k % RING, :],
                             comb_dram[XT * t + k, bass.ds(B * BT, BT)].partition_broadcast(P)
                             ).then_inc(s_cb[k % RING], 16)

            def store_block(B):
                sp.wait_ge(s_out, 2 * B + 4)
                sp.dma_start(out_blk[B], x1[:, bass.ds(B % 2, 1), :, :].rearrange("p a t d -> p (a t) d")
                             ).then_inc(s_st, 16)

            def free_residual(B):
                sp.wait_ge(s_st, 16 * B + 16)
                sp.sem_inc(s_x1free, 1)

            def tile_step(B, t, first, flush, tail, main, head):
                T = TB * (B + 1) + t
                if head:
                    load_x(T + 1)
                for k in range(XT):
                    load_row(B, t, k, first)
                    if first and k == NS - 1:
                        store_combine(T - 1)
                    if tail and not first and k == 6:
                        store_combine(T - 1)
                    if flush and k == 5:
                        store_block(B - 1)
                    if flush and k == 6:
                        free_residual(B - 1)

            with sp.Fori(1, TB) as t:
                load_x(t + 1)
                store_combine(t - 1)

            def next_context(B):
                i = sp.snap(B // BLK_B) if not isinstance(B, int) else B // BLK_B
                sp.wait_ge(s_a, TB * B + 2 * TB)
                load_context(i)

            def moe_block(B, first_block, attend, go_on):
                tile_step(B, 0, True, not first_block, True, attend, attend)
                if go_on or not attend:
                    with sp.Fori(1, TB) as t:
                        tile_step(B, t, False, False, attend, attend, attend)
                else:
                    with sp.Fori(1, TB - 1) as t:
                        tile_step(B, t, False, False, True, True, True)
                    tile_step(B, TB - 1, False, False, True, True, False)
                if go_on:
                    next_context(B)

            moe_block(0, True, True, True)
            with sp.Fori(1, N_BLK - 2) as B:
                moe_block(B, False, True, True)
            moe_block(N_BLK - 2, False, True, False)
            moe_block(N_BLK - 1, False, False, False)
            store_block(N_BLK - 1)
            sp.wait_ge(s_st, 16 * N_BLK)

        @block.gpsimd
        def _(pool):
            for i in range(NB - 1):
                nc.gpsimd.memset(w_cols[:, i * KV:i * KV + 2 * KV_K], 0.0)
            pool.drain()
            nc.gpsimd.memset(ones[:], 1.0).then_inc(s_kz, 1)
            pool.drain()
            pool.wait_ge(s_wm, 16 * 3)

            def stage(X, e, k, first_col, hi, lo, s_free, s_lo):
                raw = w_raw[:, bass.ds(e, 1), first_col:first_col + EW].rearrange("p a n -> p (a n)")
                r = k % RING
                pool.wait_ge(s_free, X + 1)
                nc.gpsimd.tensor_tensor(hi[:, r, :], raw, ones[:].broadcast_to([P, EW]), ALU.mult)
                pool.drain()
                nc.gpsimd.tensor_tensor(lo[:, r, :], raw, hi[:, r, :].bitcast(F32), ALU.subtract).then_inc(s_lo, 1)

            with pool.Fori(0, N_BLK) as B:
                with pool.Fori(0, TB) as t:
                    for k in range(XT):
                        X = NX * B + XT * t + k
                        stage(X, XT * t + k, k, 0, wu_hi, wu_lo, s_up, s_wu)
                        stage(X, XT * t + k, k, EW, wd_hi, wd_lo, s_dn, s_wd)

        @block.scalar
        def _(act):
            act.wait_ge(s_const, 16 * 8)
            nc.scalar.activation(tanh_g[:], gates[:], ACT.Tanh).then_inc(s_tanh, 1)

            def context(b, parts):
                k_h, _, v_h, _ = parts
                act.wait_ge(s_kvp, 2 * b + 3)
                for m in range(MC):
                    src = ps[:, m // 3, (m % 3) * J:(m % 3 + 1) * J]
                    nc.scalar.activation(k_h[0:64, 2 * m, :], src[0:64, :], ACT.Copy)
                    i = nc.scalar.activation(k_h[64:P, 2 * m + 1, :], src[64:P, :], ACT.Copy)
                    if m >= 2:
                        i.then_inc(s_kvh, 1)
                act.wait_ge(s_kvp, 2 * b + 4)
                for j in range(4):
                    n = min(4, NAV - 4 * j) * P
                    nc.scalar.activation(v_h[:, 512 * j:512 * j + n], ps[:, 2 + j, 0:n], ACT.Copy).then_inc(s_kvh, 1)

            act.wait_ge(s_kz, 1)
            for b in range(NB - 1):
                context(b, kv_parts(lambda c, n: w_cols_r[:, b * KV + c:b * KV + c + n]))
            context(NB - 1, (k_hi, k_lo, v_hi, v_lo))

            act.sem_inc(s_cts, 1)

            def normed_t(T, ln):
                act.wait_ge(s_xt[ln], T + 1)
                if ln == 0:
                    nc.scalar.activation(x1t_hi[:], att[:, 0, 0:EW], ACT.Copy).then_inc(s_xth, 1)
                else:
                    dst = x2t_hi[:, bass.ds(T // TB % 2, 1), :, bass.ds(T % TB * P, P)].rearrange("p a c n -> p (a c) n")
                    nc.scalar.activation(dst, att[:, 2, 0:EW].rearrange("p (c n) -> p c n", c=KC), ACT.Copy)
                    nc.scalar.activation(x2t_f[:], att[:, 2, 0:EW], ACT.Copy).then_inc(s_x2f, 1)

            def q_part(T):
                act.wait_ge(s_q, T + 1)
                nc.scalar.activation(q_hi[:], att[:, 1, :], ACT.Copy).then_inc(s_qh, 1)

            def exps(T):
                h = 0
                for bank, nh in enumerate(BANK_H):
                    act.wait_ge(s_nm, 3 * T + bank + 1)
                    for i in range(nh):
                        ins = nc.scalar.activation(prob[:, h * J:(h + 1) * J], att[:, bank, i * J:(i + 1) * J], ACT.Exp,
                                                   bias=nmax[:, h:h + 1], scale=SCALE, accum_out=psum_exp[:, h:h + 1])
                        h += 1
                    ins.then_inc(s_p, 1)

            def prob_t(T):
                for bank in range(3):
                    n = min(4, NCH - 4 * bank) * P
                    act.wait_ge(s_pt, 3 * T + bank + 1)
                    nc.scalar.activation(pt_hi[:, 512 * bank:512 * bank + n], att[:, bank, 0:n], ACT.Copy).then_inc(s_pth, 1)

            def heads(T):
                act.wait_ge(s_a, T + 1)
                nc.scalar.activation(at_hi[:], att[:, 0, :], ACT.Copy).then_inc(s_ah, 1)

            def logits_exp(T):
                act.wait_ge(s_l, T + 1)
                nc.scalar.activation(exp_l[:], att[:, 2, 320:320 + NE], ACT.Exp, scale=-1.0).then_inc(s_e, 1)

            def combine_t(T):
                act.wait_ge(s_ct, T + 1)
                act.wait_ge(s_cd, 16 * T + 16)
                nc.scalar.activation(comb_t[:], att[0:NE, 2, 384:512], ACT.Copy).then_inc(s_cts, 1)

            def hidden_hi(X, k):
                act.wait_ge(s_g, X + 4)
                nc.scalar.activation(act_hi[:, k % RING, :], act_f[:, k % RING, :], ACT.Copy).then_inc(s_gh, 1)

            def hidden(X, k):
                a = act_f[:, k % RING, :]
                act.wait_ge(s_up, X + 4)
                nc.scalar.activation(a, hid[:, k % RING, :], ACT.Relu)
                act.drain()
                nc.scalar.activation(a, a, ACT.Square).then_inc(s_sq, 1)

            def sum_scaled(B):
                act.wait_ge(s_dn, NX * B + NX + 3)
                for c in range(KC):
                    nc.scalar.activation(y_t[:, c, :], acc[:, c, :], ACT.Copy, scale=tanh_g[:, 1:2]).then_inc(s_y, 1)

            def tile_step(B, t, first, flush, tail, main, head):
                T = TB * (B + 1) + t
                for k in range(XT):
                    X = NX * B + XT * t + k
                    if not (first and not flush and k == 0):
                        hidden_hi(X - 1, (k - 1) % RING)
                    if flush and k == 2:
                        sum_scaled(B - 1)
                    hidden(X, k)
                    if main and k == 1:
                        exps(T)
                    if k == 3:
                        if tail:
                            combine_t(T - 1)
                        if main:
                            prob_t(T)
                    if main and k == 4:
                        heads(T)
                    if head and k == 6:
                        normed_t(T + 1, 0)
                    if main and k == 7:
                        normed_t(T, 1)
                    if k == 8:
                        if head:
                            q_part(T + 1)
                        if main:
                            logits_exp(T)

            def lone_tile(t, first):
                exps(t)
                prob_t(t)
                heads(t)
                normed_t(t + 1, 0)
                q_part(t + 1)
                if not first:
                    combine_t(t - 1)
                normed_t(t, 1)
                logits_exp(t)

            normed_t(0, 0)
            q_part(0)
            lone_tile(0, True)
            with act.Fori(1, TB) as t:
                lone_tile(t, False)

            def moe_block(B, first_block, attend, go_on):
                tile_step(B, 0, True, not first_block, True, attend, attend)
                if go_on or not attend:
                    with act.Fori(1, TB) as t:
                        tile_step(B, t, False, False, attend, attend, attend)
                else:
                    with act.Fori(1, TB - 1) as t:
                        tile_step(B, t, False, False, True, True, True)
                    tile_step(B, TB - 1, False, False, True, True, False)

            moe_block(0, True, True, True)
            with act.Fori(1, N_BLK - 2) as B:
                moe_block(B, False, True, True)
            moe_block(N_BLK - 2, False, True, False)
            moe_block(N_BLK - 1, False, False, False)
            hidden_hi(NX * N_BLK - 1, (NX - 1) % RING)
            sum_scaled(N_BLK - 1)

        @block.vector
        def _(dve):
            V = nc.vector
            V.memset(raw_a[:, INNER:2 * INNER], 0.0)
            V.memset(raw_b[:, INNER:2 * INNER], 0.0)
            V.memset(ctx_raw[:], 0.0)
            V.memset(mask_u8[:], 1)
            V.memset(prob[:, HJ:NCH * P], 0.0)
            V.memset(kv[:, 0:2 * KV_K].bitcast(F32), 0.0)
            V.memset(win_hi[:].bitcast(F32), 0.0)
            V.memset(win_lo[:].bitcast(F32), 0.0)
            V.memset(comb[:], 0.0)
            V.memset(row0[:], 0.0)
            dve.drain()
            V.memset(row0[0:1, :], 1.0)
            V.memset(ones_row, 1.0).then_inc(s_ones, 1)
            dve.drain()
            V.memset(nmax[:], 0.0).then_inc(s_zero, 1)
            dve.sem_inc(s_g, 3)
            dve.sem_inc(s_x1, 2)
            dve.sem_inc(s_kvl, 6)
            dve.sem_inc(s_out, 2)

            def split(dst_hi, dst_lo, raw):
                V.tensor_copy(dst_hi, raw)
                dve.drain()
                return V.tensor_tensor(dst_lo, raw, dst_hi.bitcast(F32), ALU.subtract)

            dve.wait_ge(s_const, 16 * 8)
            V.tensor_scalar(mask_add[:], mask_u8[:], -1.0, BIG, ALU.add, ALU.mult).then_inc(s_mask, 1)
            dve.wait_ge(s_wa, 16 * 7)
            split(wk_hi, wk_lo, raw_a[:, 0:2 * INNER]).then_inc(s_split, 1)
            split(wv_hi, wv_lo, raw_b[:, 0:2 * INNER])
            split(wq_hi[:], wq_lo[:], raw_c[:, 0:KC * INNER])

            def context(b, parts):
                k_h, k_l, v_h, v_l = parts
                dve.wait_ge(s_kvp, 2 * b + 2)
                split(win_hi[:, :, P:P + J], win_lo[:, :, P:P + J], ctx_raw[:, b, :, :]).then_inc(s_win, 1)
                for m in range(MC):
                    src = ps[:, m // 3, (m % 3) * J:(m % 3 + 1) * J]
                    if m == 0:
                        dve.wait_ge(s_kvh, 6 * b + 1)
                    if m == 3:
                        dve.wait_ge(s_kvh, 6 * b + 2)
                    V.tensor_tensor(k_l[0:64, 2 * m, :], src[0:64, :], k_h[0:64, 2 * m, :].bitcast(F32), ALU.subtract)
                    i = V.tensor_tensor(k_l[64:P, 2 * m + 1, :], src[64:P, :], k_h[64:P, 2 * m + 1, :].bitcast(F32), ALU.subtract)
                    if m >= 2:
                        i.then_inc(s_kvl, 1)
                for j in range(4):
                    n = min(4, NAV - 4 * j) * P
                    dve.wait_ge(s_kvh, 6 * b + 3 + j)
                    V.tensor_tensor(v_l[:, 512 * j:512 * j + n], ps[:, 2 + j, 0:n],
                                    v_h[:, 512 * j:512 * j + n].bitcast(F32), ALU.subtract).then_inc(s_kvl, 1)

            for b in range(NB - 1):
                context(b, kv_parts(lambda c, n: w_cols_r[:, b * KV + c:b * KV + c + n]))
            context(NB - 1, (k_hi, k_lo, v_hi, v_lo))
            dve.wait_ge(s_wa, 16 * 8)
            split(wo_hi[:], wo_lo[:], raw_a[:, 0:MC * D]).then_inc(s_split, 1)

            def norm(T, ln, src, dst):
                st, mv = ln_s[:, 0:6], ln_s[:, 6:8]
                ve, y, a, half = ln_s[:, 8:9], ln_s[:, 9:10], ln_s[:, 10:11], ln_s[:, 11:12]
                V.bn_stats(st, src)
                dve.drain()
                V.bn_aggr(mv, st)
                dve.drain()
                V.tensor_scalar(ve, mv[:, 1:2], EPS, None, ALU.add)
                V.tensor_scalar(half, mv[:, 1:2], EPS, -0.5, ALU.add, ALU.mult)
                dve.drain()
                V.tensor_scalar(ln_i[:, 0:1], ve.bitcast(I32), 1, None, ALU.logical_shift_right)
                dve.drain()
                V.tensor_scalar(y.bitcast(I32), ln_i[:, 0:1], -1.0, RSQRT_MAGIC, ALU.mult, ALU.add)
                dve.drain()
                for _ in range(3):
                    V.scalar_tensor_tensor(a, y, half, y, ALU.mult, ALU.mult)
                    dve.drain()
                    V.scalar_tensor_tensor(y, a, 1.5, y, ALU.add, ALU.mult)
                    dve.drain()
                V.tensor_scalar(dst, src, mv[:, 0:1], y, ALU.subtract, ALU.mult).then_inc(s_xn[ln], 1)

            def half_of_x(T):
                return x_in[:, bass.ds(T % 2, 1), :].rearrange("p a d -> p (a d)")

            def residual_of(T):
                return x1[:, bass.ds(T // TB % 2, 1), bass.ds(T % TB, 1), :].rearrange("p a t d -> p (a t d)")

            def norm_in(T):
                dve.wait_ge(s_x, 16 * T + 16)
                norm(T, 0, half_of_x(T), x_n1[:])

            def normed_t(T, ln):
                dve.wait_ge((s_xth, s_x2f)[ln], T + 1)
                if ln == 0:
                    V.tensor_tensor(x1t_lo[:], att[:, 0, 0:EW], x1t_hi[:].bitcast(F32), ALU.subtract).then_inc(s_xtl[ln], 1)
                else:
                    par, col = T // TB % 2, T % TB * P
                    hi = x2t_hi[:, bass.ds(par, 1), :, bass.ds(col, P)].rearrange("p a c n -> p (a c) n")
                    lo = x2t_lo[:, bass.ds(par, 1), :, bass.ds(col, P)].rearrange("p a c n -> p (a c) n")
                    V.tensor_tensor(lo, att[:, 2, 0:EW].rearrange("p (c n) -> p c n", c=KC), hi.bitcast(F32),
                                    ALU.subtract).then_inc(s_xtl[ln], 1)

            def q_part(T):
                dve.wait_ge(s_qh, T + 1)
                V.tensor_tensor(q_lo[:], att[:, 1, :], q_hi[:].bitcast(F32), ALU.subtract).then_inc(s_ql, 1)

            def maxima(T):
                h = 0
                for bank, nh in enumerate(BANK_H):
                    dve.wait_ge(s_s, 3 * T + bank + 1)
                    V.tensor_reduce(rsum[:, h:h + nh], att[:, bank, 0:nh * J].rearrange("p (a j) -> p a j", a=nh),
                                    op=ALU.max, axis=AX_X)
                    dve.drain()
                    V.tensor_scalar(nmax[:, h:h + nh], rsum[:, h:h + nh], -SCALE, None, ALU.mult).then_inc(s_nm, 1)
                    h += nh

            def normalise(T):
                dve.wait_ge(s_p, 3 * T + 3)
                V.reciprocal(rsum[:], psum_exp[:])
                dve.drain()
                p3 = prob[:, 0:HJ].rearrange("p (h j) -> p h j", h=NH)
                V.tensor_tensor(p3, p3, rsum[:].unsqueeze(2).broadcast_to([P, NH, J]), ALU.mult).then_inc(s_pn, 1)

            def prob_t(T):
                for bank in range(3):
                    n = min(4, NCH - 4 * bank) * P
                    dve.wait_ge(s_pth, 3 * T + bank + 1)
                    V.tensor_tensor(pt_lo[:, 512 * bank:512 * bank + n], att[:, bank, 0:n],
                                    pt_hi[:, 512 * bank:512 * bank + n].bitcast(F32), ALU.subtract).then_inc(s_ptl, 1)

            def heads(T):
                dve.wait_ge(s_ah, T + 1)
                V.tensor_tensor(at_lo[:], att[:, 0, :], at_hi[:].bitcast(F32), ALU.subtract).then_inc(s_al, 1)

            def residual(T, blk):
                dve.wait_ge(s_o, T + 1)
                dve.wait_ge(s_x1free, blk)
                V.tensor_tensor(x_n2, att[:, 1, 0:D], bias_o[:], ALU.add)
                dve.drain()
                V.scalar_tensor_tensor(residual_of(T), x_n2, tanh_g[:, 0:1], half_of_x(T), ALU.mult, ALU.add).then_inc(s_x1, 1)

            def norm_out(T):
                dve.drain()
                norm(T, 1, residual_of(T), x_n2)

            best, idx_g = grp[:, 56:64], grp[:, 64:72]
            low = grp[:, 48:56]

            def router_groups(T):
                dve.wait_ge(s_e, T + 1)
                V.tensor_scalar(score[:], exp_l[:], 1.0, None, ALU.add)
                dve.drain()
                V.reciprocal(score[:], score[:])
                dve.drain()
                V.tensor_tensor(biased[:], score[:], bias_e[:], ALU.add)
                dve.drain()
                mx, mn = grp[:, 0:16], grp[:, 16:32]
                V.tensor_tensor(mx, biased[:, 0:NE:2], biased[:, 1:NE:2], ALU.max)
                V.tensor_tensor(mn, biased[:, 0:NE:2], biased[:, 1:NE:2], ALU.min)
                dve.drain()
                first, other = grp[:, 32:40], grp[:, 40:48]
                V.tensor_tensor(first, mx[:, 0:16:2], mx[:, 1:16:2], ALU.max)
                V.tensor_tensor(other, mx[:, 0:16:2], mx[:, 1:16:2], ALU.min)
                V.tensor_tensor(low, mn[:, 0:16:2], mn[:, 1:16:2], ALU.max)
                dve.drain()
                V.tensor_tensor(other, other, low, ALU.max)
                dve.drain()
                V.tensor_tensor(first, first, other, ALU.add)
                dve.drain()

            def router_masked():
                first = grp[:, 32:40]
                V.max(best, first)
                dve.drain()
                V.max_index(grp_i[:, 0:8], best, first)
                dve.drain()
                V.tensor_copy(idx_g, grp_i[:, 0:8])
                dve.drain()
                V.tensor_tensor(hot_g[:], iota_f[:, 0:NG].unsqueeze(1).broadcast_to([P, TOPG, NG]),
                                idx_g[:, 0:TOPG].unsqueeze(2).broadcast_to([P, TOPG, NG]), ALU.is_equal)
                dve.drain()
                V.tensor_reduce(low, hot_g[:].rearrange("p k g -> p g k"), op=ALU.max, axis=AX_X)
                dve.drain()
                V.tensor_tensor(masked[:].rearrange("p (g e) -> p g e", g=NG), biased[:].rearrange("p (g e) -> p g e", g=NG),
                                low.unsqueeze(2).broadcast_to([P, NG, GE]), ALU.mult)
                dve.drain()
                V.tensor_scalar(masked[:], masked[:], 0.0, None, ALU.add)
                dve.drain()

            def router_weights():
                V.max(best, masked[:])
                dve.drain()
                V.max_index(grp_i[:, 8:16], best, masked[:])
                dve.drain()
                V.tensor_copy(idx_g, grp_i[:, 8:16])
                dve.drain()
                V.tensor_tensor(hot[:], iota_f[:].unsqueeze(1).broadcast_to([P, TOPK, NE]),
                                idx_g[:, 0:TOPK].unsqueeze(2).broadcast_to([P, TOPK, NE]), ALU.is_equal)
                dve.drain()
                V.tensor_reduce(sel[:], hot[:].rearrange("p k e -> p e k"), op=ALU.max, axis=AX_X)
                dve.drain()
                total = grp[:, 72:73]
                V.tensor_tensor_reduce(out=weighted[:], in0=sel[:], in1=score[:], scale=1.0, scalar=0.0,
                                       op0=ALU.mult, op1=ALU.add, accum_out=total)
                dve.drain()
                V.tensor_scalar(total, total, 1e-20, None, ALU.add)
                dve.drain()
                V.reciprocal(total, total)
                dve.drain()
                V.tensor_scalar(comb[:, 0:NE], weighted[:], total, ROUTED_SCALE, ALU.mult, ALU.mult).then_inc(s_c, 1)

            def hidden_lo(X, k):
                r = k % RING
                dve.wait_ge(s_gh, X + 1)
                V.tensor_tensor(act_lo[:, r, :], act_f[:, r, :], act_hi[:, r, :].bitcast(F32), ALU.subtract).then_inc(s_gl, 1)

            def hidden(X, B, t, k):
                r = k % RING
                dve.wait_ge(s_sq, X + 1)
                dve.wait_ge(s_cb[r], 16 * ((NX // RING) * B + (XT // RING) * t + k // RING + 1))
                V.tensor_tensor(act_f[:, r, :], act_f[:, r, :], comb_b[:, r, :], ALU.mult).then_inc(s_g, 1)

            def add_sum(B):
                for j in range(2):
                    dst = x1[:, bass.ds(B % 2, 1), 2 * j:2 * j + 2, :].rearrange("p a t d -> p (a t d)")
                    dve.wait_ge(s_yt, 2 * B + j + 1)
                    V.tensor_tensor(dst, acc[:, j, :], dst, ALU.add).then_inc(s_out, 1)

            def tile_step(B, t, first, flush, tail, main, head):
                T = TB * (B + 1) + t
                for k in range(XT):
                    X = NX * B + XT * t + k
                    if not (first and not flush and k == 0):
                        hidden_lo(X - 1, (k - 1) % RING)
                    if tail and k == 2:
                        router_weights()
                    if flush and k == 2:
                        add_sum(B - 1)
                    hidden(X, B, t, k)
                    if k == 0:
                        if tail:
                            router_groups(T - 1)
                        if main:
                            maxima(T)
                    if tail and k == 1:
                        router_masked()
                    if main and k == 2:
                        normalise(T)
                    if main and k == 3:
                        prob_t(T)
                    if head and k == 4:
                        norm_in(T + 1)
                    if main and k == 4:
                        heads(T)
                    if main and k == 5:
                        residual(T, B + 1)
                        norm_out(T)
                    if head and k == 6:
                        normed_t(T + 1, 0)
                    if main and k == 7:
                        normed_t(T, 1)
                    if head and k == 8:
                        q_part(T + 1)

            def lone_tile(t, first):
                maxima(t)
                if not first:
                    router_groups(t - 1)
                normalise(t)
                if not first:
                    router_masked()
                prob_t(t)
                norm_in(t + 1)
                heads(t)
                residual(t, 1)
                normed_t(t + 1, 0)
                norm_out(t)
                q_part(t + 1)
                if not first:
                    router_weights()
                normed_t(t, 1)

            dve.wait_ge(s_tanh, 1)
            norm_in(0)
            normed_t(0, 0)
            q_part(0)
            lone_tile(0, True)
            with dve.Fori(1, TB) as t:
                lone_tile(t, False)

            def moe_block(B, first_block, attend, go_on):
                tile_step(B, 0, True, not first_block, True, attend, attend)
                if go_on or not attend:
                    with dve.Fori(1, TB) as t:
                        tile_step(B, t, False, False, attend, attend, attend)
                else:
                    with dve.Fori(1, TB - 1) as t:
                        tile_step(B, t, False, False, True, True, True)
                    tile_step(B, TB - 1, False, False, True, True, False)

            moe_block(0, True, True, True)
            with dve.Fori(1, N_BLK - 2) as B:
                moe_block(B, False, True, True)
            moe_block(N_BLK - 2, False, True, False)
            moe_block(N_BLK - 1, False, False, False)
            hidden_lo(NX * N_BLK - 1, (NX - 1) % RING)
            add_sum(N_BLK - 1)

        @block.tensor
        def _(pe):
            pe.sem_inc(s_up, 3)
            pe.sem_inc(s_dn, 3)
            pe.sem_inc(s_kvp, 2)
            pe.wait_ge(s_split, 1)
            with pe.Fori(0, NB) as b:
                pe.wait_ge(s_win, b + 1)
                pe.wait_ge(s_kvl, 6 * b + 6)
                for m in range(MC):
                    o = ps[:, m // 3, (m % 3) * J:(m % 3 + 1) * J]
                    for c in range(2):
                        w = slice(c * INNER + m * P, c * INNER + (m + 1) * P)
                        ins = three(o, wk_hi[:, w], wk_lo[:, w], win_hi[:, c, P:P + J], win_lo[:, c, P:P + J], c == 0, c == 1)
                ins.then_inc(s_kvp, 1)
                for n, (m, ch) in enumerate(AV):
                    for i in range(2):
                        h = 2 * m + i
                        at = P + min(max(ch * P - h * J, -P), J)
                        o = ps[:, 2 + n // 4, n % 4 * P + i * DH:n % 4 * P + (i + 1) * DH]
                        for c in range(2):
                            w = slice(c * INNER + h * DH, c * INNER + (h + 1) * DH)
                            ins = three(o, win_hi[:, c, at:at + P], win_lo[:, c, at:at + P], wv_hi[:, w], wv_lo[:, w], c == 0, c == 1)
                ins.then_inc(s_kvp, 1)
            pe.wait_ge(s_kvl, 6 * NB + 6)
            pe.wait_ge(s_split, 2)
            pe.wait_ge(s_mask, 1)

            def normed_t(T, ln):
                x_n = (x_n1, x_n2)[ln]
                pe.wait_ge(s_xn[ln], T + 1)
                if ln == 1:
                    pe.wait_ge(s_cts, T + 1)
                for c in range(KC):
                    ins = nc.tensor.transpose(att[:, 2 * ln, c * P:(c + 1) * P], x_n[:, c * P:(c + 1) * P], ident[:])
                ins.then_inc(s_xt[ln], 1)

            def q_part(T):
                pe.wait_ge(s_xtl[0], T + 1)
                pe.wait_ge(s_x1, T + 2)
                for m in range(MC):
                    for c in range(KC):
                        w = slice(c * INNER + m * P, c * INNER + (m + 1) * P)
                        f = slice(c * P, (c + 1) * P)
                        ins = three(att[:, 1, m * P:(m + 1) * P], wq_hi[:, w], wq_lo[:, w], x1t_hi[:, f], x1t_lo[:, f], c == 0, c == KC - 1)
                ins.then_inc(s_q, 1)

            def scores(T, b):
                pe.wait_ge(s_ql, T + 1)
                if not (isinstance(T, int) and T == 0):
                    pe.wait_ge(s_e, T)
                for bank, col, heads_in in SCORES:
                    if col == 0:
                        nh = BANK_H[bank]
                        nc.tensor.matmul(att[:, bank, 0:nh * J].rearrange("p (a j) -> p a j", a=nh), row0[:],
                                         mask_add[:, bass.ds(b, 1), :].broadcast_to([P, nh, J]),
                                         start=True, stop=False, skip_group_check=True)
                    h, n = heads_in[0], len(heads_in)
                    f = slice(h // 2 * P, (h // 2 + 1) * P)
                    keys = [a[:, h:h + n, :].rearrange("p a j -> p (a j)") for a in (k_hi, k_lo)]
                    ins = three(att[:, bank, col:col + n * J], q_hi[:, f], q_lo[:, f], keys[0], keys[1], False, True)
                    if heads_in[-1] + 1 in (3, 6, 8):
                        ins.then_inc(s_s, 1)

            def prob_t(T, tail):
                pe.wait_ge(s_pn, T + 1)
                if tail:
                    combine_t(T - 1)
                for c in range(NCH):
                    if tail and c == 8:
                        pe.wait_ge(s_cts, T + 1)
                    ins = nc.tensor.transpose(att[:, c // 4, c % 4 * P:(c % 4 + 1) * P], prob[:, c * P:(c + 1) * P], ident[:])
                    if c % 4 == 3 or c == NCH - 1:
                        ins.then_inc(s_pt, 1)

            def heads(T):
                pe.wait_ge(s_ptl, 3 * T + 3)
                for n, (m, c) in enumerate(AV):
                    f, r = slice(n * P, (n + 1) * P), slice(c * P, (c + 1) * P)
                    ins = three(att[:, 0, m * P:(m + 1) * P], v_hi[:, f], v_lo[:, f], pt_hi[:, r], pt_lo[:, r],
                                n == 0 or AV[n - 1][0] != m, n == NAV - 1 or AV[n + 1][0] != m)
                ins.then_inc(s_a, 1)

            def attn_out(T):
                pe.wait_ge(s_al, T + 1)
                for m in range(MC):
                    f, w = slice(m * P, (m + 1) * P), slice(m * D, (m + 1) * D)
                    ins = three(att[:, 1, 0:D], at_hi[:, f], at_lo[:, f], wo_hi[:, w], wo_lo[:, w], m == 0, m == MC - 1)
                ins.then_inc(s_o, 1)

            def logits(T):
                pe.wait_ge(s_xtl[1], T + 1)
                for c in range(KC):
                    ins = nc.tensor.matmul(att[:, 2, 320:320 + NE], x2t_f[:, c * P:(c + 1) * P], gate_w[:, c, :],
                                           start=c == 0, stop=c == KC - 1, skip_group_check=True)
                ins.then_inc(s_l, 1)

            def combine_t(T):
                pe.wait_ge(s_c, T + 1)
                pe.wait_ge(s_cts, T + 1)
                nc.tensor.transpose(att[:, 2, 384:512], comb[:], ident[:]).then_inc(s_ct, 1)

            def up(X, B, k):
                r = k % RING
                pe.wait_ge(s_wu, X + 1)
                for c in range(KC):
                    w = slice(c * P, (c + 1) * P)
                    hi = x2t_hi[:, bass.ds(B % 2, 1), c, :].rearrange("p a n -> p (a n)")
                    lo = x2t_lo[:, bass.ds(B % 2, 1), c, :].rearrange("p a n -> p (a n)")
                    ins = three(hid[:, r, :], wu_hi[:, r, w], wu_lo[:, r, w], hi, lo, c == 0, c == KC - 1)
                ins.then_inc(s_up, 1)

            def down(X, k, start, stop):
                r = k % RING
                pe.wait_ge(s_wd, X + 1)
                pe.wait_ge(s_gl, X + 1)
                for c in range(KC):
                    w = slice(c * P, (c + 1) * P)
                    ins = three(acc[:, c, :], wd_hi[:, r, w], wd_lo[:, r, w], act_hi[:, r, :], act_lo[:, r, :], start, stop)
                ins.then_inc(s_dn, 1)

            def sum_t(B):
                pe.wait_ge(s_y, 2 * B + 2)
                for i in range(TB):
                    for c in range(KC):
                        ins = nc.tensor.transpose(acc[:, i // 2, i % 2 * D + c * P:i % 2 * D + (c + 1) * P],
                                                  y_t[:, c, i * P:(i + 1) * P], ident[:])
                    if i % 2:
                        ins.then_inc(s_yt, 1)

            def tile_step(B, t, first, flush, tail, main, head):
                T = TB * (B + 1) + t
                for k in range(XT):
                    X = NX * B + XT * t + k
                    up(X, B, k)
                    if flush and k == 2:
                        sum_t(B - 1)
                        pe.wait_ge(s_out, 2 * B + 2)
                    if not first or flush or k >= 2:
                        down(X - 2, (k - 2) % RING, first and k == 2, first and k == 1)
                    if main and k == 0:
                        if not (isinstance(B, int) and B == 0):
                            pe.wait_ge(s_k, 16 * B)
                        scores(T, (B + 1) // BLK_B)
                    if k == 3:
                        if main:
                            prob_t(T, tail)
                        elif tail:
                            combine_t(T - 1)
                    if main and k == 4:
                        if not (isinstance(B, int) and B == 0):
                            pe.wait_ge(s_v, 16 * B)
                        heads(T)
                    if main and k == 5:
                        attn_out(T)
                    if head and k == 6:
                        normed_t(T + 1, 0)
                    if main and k == 7:
                        normed_t(T, 1)
                    if k == 8:
                        if head:
                            q_part(T + 1)
                        if main:
                            logits(T)

            def lone_tile(t, first):
                scores(t, 0)
                prob_t(t, False)
                heads(t)
                attn_out(t)
                normed_t(t + 1, 0)
                q_part(t + 1)
                if not first:
                    combine_t(t - 1)
                normed_t(t, 1)
                logits(t)

            normed_t(0, 0)
            q_part(0)
            lone_tile(0, True)
            with pe.Fori(1, TB) as t:
                lone_tile(t, False)

            def moe_block(B, first_block, attend, go_on):
                pe.wait_ge(s_xtl[1], TB * B + TB)
                tile_step(B, 0, True, not first_block, True, attend, attend)
                if go_on or not attend:
                    with pe.Fori(1, TB) as t:
                        tile_step(B, t, False, False, attend, attend, attend)
                else:
                    with pe.Fori(1, TB - 1) as t:
                        tile_step(B, t, False, False, True, True, True)
                    tile_step(B, TB - 1, False, False, True, True, False)

            moe_block(0, True, True, True)
            with pe.Fori(1, N_BLK - 2) as B:
                moe_block(B, False, True, True)
            moe_block(N_BLK - 2, False, True, False)
            moe_block(N_BLK - 1, False, False, False)
            for e in (NX - 2, NX - 1):
                down(NX * (N_BLK - 1) + e, e, False, e == NX - 1)
            sum_t(N_BLK - 1)


_INS = ["x", "ctx_t", "mask", "g_xattn", "g_ffn", "w_q", "w_k", "w_v", "w_o", "b_o", "gate_t", "e_bias",
        "w_moe", "eye", "iota"]


def kernel(x, ctx_768, mask_BxS2_bk0, g_xattn, g_ffn, L0_xattn_W_q, L0_xattn_W_k, L0_xattn_W_v, L0_xattn_W_o,
           L0_xattn_b_o, L0_ffn_gate_w, L0_ffn_e_bias, L0_ffn_up_w, L0_ffn_down_w, L0_ffn_shared_up_w,
           L0_ffn_shared_down_w):
    import numpy as np
    import concourse.bacc as bacc
    from concourse.bass_utils import run_bass_kernel_spmd

    x = np.asarray(x)
    shape = x.shape
    d = shape[-1]
    up, down = np.asarray(L0_ffn_up_w), np.asarray(L0_ffn_down_w)
    part = up.shape[1]
    sup = np.asarray(L0_ffn_shared_up_w).reshape(-1, part, d)
    sdn = np.asarray(L0_ffn_shared_down_w).reshape(d, -1, part).transpose(1, 0, 2)
    ups = np.concatenate([sup, up])
    downs = np.concatenate([sdn, down])
    ups = ups.transpose(2, 0, 1).reshape(d // P, P, -1, part).transpose(1, 2, 0, 3).reshape(P, -1, d)
    downs = downs.transpose(2, 0, 1)
    arrays = {
        "x": x.reshape(-1, d),
        "ctx_t": np.roll(np.asarray(ctx_768), -1, axis=0).transpose(0, 2, 1),
        "mask": np.asarray(mask_BxS2_bk0),
        "g_xattn": np.asarray(g_xattn), "g_ffn": np.asarray(g_ffn),
        "w_q": np.asarray(L0_xattn_W_q), "w_k": np.asarray(L0_xattn_W_k), "w_v": np.asarray(L0_xattn_W_v),
        "w_o": np.asarray(L0_xattn_W_o), "b_o": np.asarray(L0_xattn_b_o),
        "gate_t": np.asarray(L0_ffn_gate_w).T, "e_bias": np.asarray(L0_ffn_e_bias),
        "w_moe": np.concatenate([ups, downs], axis=2),
        "eye": np.eye(P, dtype=np.float32),
        "iota": np.tile(np.arange(len(L0_ffn_gate_w), dtype=np.float32), (P, 1)),
    }
    nc = bacc.Bacc("TRN2", target_bir_lowering=False, num_devices=1)
    feeds, args = {}, []
    for name in _INS:
        a = np.ascontiguousarray(arrays[name])
        feeds[f"in_{name}"] = a
        args.append(nc.dram_tensor(f"in_{name}", a.shape, mybir.dt.from_np(a.dtype), kind="ExternalInput").ap())
    out = nc.dram_tensor("out", arrays["x"].shape, F32, kind="ExternalOutput").ap()
    flamingo_block(nc, *args, out)
    r = run_bass_kernel_spmd(nc, [feeds], core_ids=[0])
    return r.results[0]["out"].reshape(shape)
```

```python
from contextlib import ExitStack

import concourse.bass as bass
from concourse import mybir

F32 = mybir.dt.float32
F32R = mybir.dt.float32r
BF16 = mybir.dt.bfloat16
I32 = mybir.dt.int32
U32 = mybir.dt.uint32
U8 = mybir.dt.uint8
ALU = mybir.AluOpType
ACT = mybir.ActivationFunctionType
AX_X = mybir.AxisListType.X

P = 128
EPS = 1e-5
BIG = 3.0e38
RSQRT_MAGIC = 1597463007.0
ROUTED_SCALE = 2.5


def flamingo_block(nc, x, ctx_t, mask, g_xattn, g_ffn, w_qt, w_k, w_v, w_o, b_o, gate_t, e_bias,
                   w_moe, eye, iota, out):
    n_tok, D = x.shape
    NB, CD, J = ctx_t.shape
    INNER = w_qt.shape[0]
    DH = 64
    NH = INNER // DH
    SCALE = float(DH) ** -0.5
    KC = D // P
    MC = INNER // P
    NE = e_bias.shape[0]
    NG, GE, TOPG, TOPK = 8, NE // 8, 4, 6
    NX = w_moe.shape[1]
    NS = NX - NE
    EW = KC * P
    BT = 512
    TB = BT // P
    N_BLK = n_tok // BT
    XT = NX // TB
    BLK_B = n_tok // NB // BT
    BANK_H = (3, 3, 2)
    HJ = NH * J
    NCH = -(-HJ // P)
    AV = [(m, c) for m in range(MC) for c in range(NCH)
          if c * P < (2 * m + 2) * J and (c + 1) * P > 2 * m * J]
    WIN = P + 2 * J + P
    MAP_A, MAP_U = KC * HJ, NCH * D
    MAPS = 2 * MAP_A + 2 * MAP_U
    MAP_BANKS = (4, 5, 6, 7, 0, 1, 2, 3, 4, 5, 6)
    NMB = len(MAP_BANKS)
    RING = 3
    assert XT % RING == 0 and NX == TB * XT
    assert MAPS + 2 * HJ + 2 * MC * WIN <= NX * 2 * EW

    x_tiles = x.rearrange("(t p) d -> t p d", p=P)
    out_blk = out.rearrange("(b t p) d -> b p t d", p=P, t=TB)
    comb_dram = nc.dram_tensor("combine_weights", [NX, n_tok], F32, kind="Internal").ap()
    maps_dram = nc.dram_tensor("context_maps", [NB - 1, P, MAPS], F32, kind="Internal").ap()

    with ExitStack() as ctx:
        def sb(name, shape, dt):
            return ctx.enter_context(nc.sbuf_tensor(name, shape, dt))

        def sem(name):
            return ctx.enter_context(nc.semaphore(name))

        ps = ctx.enter_context(nc.psum_tensor("ps", [P, 8, 512], F32))
        acc = ps[:, 0:2, :]
        hid = ps[:, 2:5, :]
        att = ps[:, 5:8, :]

        w_raw = sb("w_raw", [P, NX, 2 * EW], F32)
        wu_hi = sb("wu_hi", [P, RING, EW], F32R)
        wu_lo = sb("wu_lo", [P, RING, EW], F32R)
        wd_hi = sb("wd_hi", [P, RING, EW], F32R)
        wd_lo = sb("wd_lo", [P, RING, EW], F32R)
        maps = sb("maps", [P, MAPS], F32R)
        a_hi, a_lo = [maps[:, i * MAP_A:(i + 1) * MAP_A].rearrange("p (c n) -> p c n", c=KC) for i in range(2)]
        u_hi, u_lo = [maps[:, 2 * MAP_A + i * MAP_U:2 * MAP_A + (i + 1) * MAP_U].rearrange("p (c n) -> p c n", c=NCH)
                      for i in range(2)]
        ident = sb("ident", [P, P], F32)
        iota_f = sb("iota_f", [P, NE], F32)
        bias_e = sb("bias_e", [P, NE], F32)
        bias_o = sb("bias_o", [P, D], F32)
        gates = sb("gates", [P, 2], F32)
        tanh_g = sb("tanh_g", [P, 2], F32)
        mask_u8 = sb("mask_u8", [P, NB, J], U8)
        mask_add = sb("mask_add", [P, NB, J], BF16)
        row0 = sb("row0", [P, P], BF16)
        ones = sb("ones", [P, 1], F32)
        y_t = sb("y_t", [P, KC, BT], F32)
        ones_row = y_t[0:NS, 1, :]
        gate_w = sb("gate_w", [P, KC, NE], F32)
        x_in = sb("x_in", [P, 2, D], F32)
        x_n1 = sb("x_n1", [P, D], F32)
        x_n2 = y_t[:, 0, 0:D]
        x1t_hi = sb("x1t_hi", [P, EW], F32R)
        x1t_lo = sb("x1t_lo", [P, EW], F32R)
        prob = sb("prob", [P, NCH * P], F32)
        pt_hi = sb("pt_hi", [P, NCH * P], F32R)
        pt_lo = sb("pt_lo", [P, NCH * P], F32R)
        nmax = sb("nmax", [P, NH], F32)
        psum_exp = sb("psum_exp", [P, NH], F32)
        rsum = sb("rsum", [P, NH], F32)
        ln_s = sb("ln_s", [P, 16], F32)
        ln_i = sb("ln_i", [P, 2], I32)
        x1 = sb("x1", [P, 2, TB, D], F32)
        x2t_hi = sb("x2t_hi", [P, 2, KC, BT], F32R)
        x2t_lo = sb("x2t_lo", [P, 2, KC, BT], F32R)
        x2t_f = sb("x2t_f", [P, EW], F32)
        exp_l = sb("exp_l", [P, NE], F32)
        score = sb("score", [P, NE], F32)
        biased = sb("biased", [P, NE], F32)
        grp = sb("grp", [P, 96], F32)
        grp_i = sb("grp_i", [P, 16], U32)
        hot_g = sb("hot_g", [P, TOPG, NG], F32)
        masked = sb("masked", [P, NE], F32)
        hot = sb("hot", [P, TOPK, NE], F32)
        sel = sb("sel", [P, NE], F32)
        weighted = sb("weighted", [P, NE], F32)
        comb = sb("comb", [P, P], F32)
        comb_t = sb("comb_t", [NE, P], F32)
        comb_b = sb("comb_b", [P, RING, BT], F32)
        act_f = sb("act_f", [P, RING, BT], F32)
        act_hi = sb("act_hi", [P, RING, BT], F32R)
        act_lo = sb("act_lo", [P, RING, BT], F32R)

        w_cols = w_raw[:, :, :].rearrange("p e n -> p (e n)")
        w_cols_r = w_cols.bitcast(F32R)
        staged = w_cols_r[:, 0:MAPS]
        kv_0 = MAPS
        k_hi, k_lo = [w_cols_r[:, kv_0 + i * HJ:kv_0 + (i + 1) * HJ].rearrange("p (h j) -> p h j", h=NH) for i in range(2)]
        v_hi, v_lo = [w_cols_r[:, kv_0 + 2 * HJ + i * MC * WIN:kv_0 + 2 * HJ + (i + 1) * MC * WIN]
                      .rearrange("p (m w) -> p m w", m=MC) for i in range(2)]
        raw_a = act_f[:, :, :].rearrange("p a b -> p (a b)")
        raw_b = comb_b[:, :, :].rearrange("p a b -> p (a b)")
        raw_c = x1[:, :, :, :].rearrange("p a t d -> p (a t d)")
        ctx_raw = prob[:, 0:NB * 2 * J].rearrange("p (b c j) -> p b c j", b=NB, c=2)
        flat_hi = act_hi[:, :, :].rearrange("p a b -> p (a b)")
        flat_lo = act_lo[:, :, :].rearrange("p a b -> p (a b)")
        wk_hi, wk_lo = flat_hi[:, 0:2 * INNER], flat_lo[:, 0:2 * INNER]
        ctx_hi, ctx_lo = [f[:, 2 * INNER:2 * INNER + 2 * J].rearrange("p (c j) -> p c j", c=2) for f in (flat_hi, flat_lo)]
        wv_hi, wv_lo = [a[:, 1, :, :].rearrange("p a b -> p (a b)") for a in (x2t_hi, x2t_lo)]
        wo_hi, wo_lo = [a[:, 0, :, :].rearrange("p a b -> p (a b)") for a in (x2t_hi, x2t_lo)]
        wq_hi, wq_lo = pt_hi[:, 0:MC * D], pt_lo[:, 0:MC * D]

        s_zero = sem("rows_cleared")
        s_kz = sem("key_rows_cleared")
        s_const = sem("constants_loaded")
        s_wa = sem("attention_weights_loaded")
        s_wm = sem("expert_weights_loaded")
        s_ones = sem("ones_ready")
        s_mask = sem("mask_ready")
        s_tanh = sem("tanh_ready")
        s_split = sem("attention_weights_split")
        s_win = sem("context_split")
        s_kvp = sem("keys_values_in_psum")
        s_kvh = sem("keys_values_hi")
        s_kvl = sem("keys_values_lo")
        s_mp = sem("maps_in_psum")
        s_mh = sem("maps_hi")
        s_ml = sem("maps_lo")
        s_ms = sem("maps_stored")
        s_x = sem("x_loaded")
        s_am = sem("score_maps_loaded")
        s_um = sem("output_maps_loaded")
        s_xn = [sem(f"normed_{i}") for i in (1, 2)]
        s_xt = [sem(f"normed_{i}_t_psum") for i in (1, 2)]
        s_xth = sem("normed_1_t_hi")
        s_xtl = [sem(f"normed_{i}_t_lo") for i in (1, 2)]
        s_s = sem("scores_psum")
        s_nm = sem("max_ready")
        s_p = sem("exp_ready")
        s_pn = sem("prob_ready")
        s_pt = sem("prob_t_psum")
        s_pth = sem("prob_t_hi")
        s_ptl = sem("prob_t_lo")
        s_o = sem("attn_out_psum")
        s_x1 = sem("residual_ready")
        s_x2f = sem("normed_2_t_hi_and_copy")
        s_l = sem("logits_psum")
        s_e = sem("logits_exp")
        s_c = sem("combine_ready")
        s_ct = sem("combine_t_psum")
        s_cts = sem("combine_t_sbuf")
        s_cd = sem("combine_stored")
        s_wu = sem("up_staged")
        s_wd = sem("down_staged")
        s_cb = [sem(f"combine_row_{i}") for i in range(RING)]
        s_up = sem("hidden_psum")
        s_sq = sem("squared")
        s_g = sem("weighted_hidden")
        s_gh = sem("hidden_hi")
        s_gl = sem("hidden_lo")
        s_dn = sem("down_done")
        s_y = sem("sum_t_sbuf")
        s_yt = sem("sum_psum")
        s_out = sem("output_ready")
        s_st = sem("output_stored")
        s_x1free = sem("residual_free")

        block = ctx.enter_context(nc.Block())

        def three(o, l_hi, l_lo, r_hi, r_lo, start, stop):
            nc.tensor.matmul(o, l_hi, r_lo, start=start, stop=False, skip_group_check=True)
            nc.tensor.matmul(o, l_lo, r_hi, start=False, stop=False, skip_group_check=True)
            return nc.tensor.matmul(o, l_hi, r_hi, start=False, stop=stop, skip_group_check=True)

        def map_columns(n):
            if n < 6:
                return n // 3 * HJ + sum(BANK_H[:n % 3]) * J, BANK_H[n % 3] * J
            return 2 * MAP_A + (n - 6) * 2 * D, 2 * D


        @block.sync
        def _(sp):
            sp.sem_inc(s_x1free, 1)
            sp.sem_inc(s_ms, 32)
            half = CD - P
            for dst, src in (
                (raw_a[:, 0:INNER], w_k[0:P, :]), (raw_a[0:half, INNER:2 * INNER], w_k[P:CD, :]),
                (ctx_raw[:, :, 0, :], ctx_t[:, 0:P, :].rearrange("b p j -> p b j")),
                (ctx_raw[0:half, :, 1, :], ctx_t[:, P:CD, :].rearrange("b p j -> p b j")),
                (raw_b[:, 0:INNER], w_v[0:P, :]), (raw_b[0:half, INNER:2 * INNER], w_v[P:CD, :]),
                (raw_c[:, 0:MC * D].rearrange("p (c n) -> p c n", c=MC), w_qt.rearrange("(c p) n -> p c n", p=P)),
                (raw_c[:, MC * D:2 * MC * D].rearrange("p (c n) -> p c n", c=MC), w_o.rearrange("(c p) n -> p c n", p=P)),
            ):
                sp.dma_start(dst, src).then_inc(s_wa, 16)
            for dst, src in ((ident[:], eye), (iota_f[:], iota),
                             (bias_e[:], e_bias.partition_broadcast(P)),
                             (bias_o[:], b_o.partition_broadcast(P)),
                             (gates[:, 0:1], g_xattn.partition_broadcast(P)),
                             (gates[:, 1:2], g_ffn.partition_broadcast(P)),
                             (gate_w[:], gate_t.rearrange("(c p) e -> p c e", p=P))):
                sp.dma_start(dst, src).then_inc(s_const, 16)
            sp.wait_ge(s_zero, 1)
            sp.dma_start(mask_u8[0:1, :, :], mask.rearrange("(a b) j -> a b j", a=1)).then_inc(s_const, 16)
            sp.wait_ge(s_ones, 1)
            sp.dma_start(comb_dram[0:NS, :].rearrange("e (a n) -> e a n", n=512),
                         ones_row.unsqueeze(1).broadcast_to([NS, n_tok // 512, 512])).then_inc(s_cd, 16)

            def load_x(T):
                sp.wait_ge(s_x1, T + 1)
                sp.dma_start(x_in[:, bass.ds(T % 2, 1), :].rearrange("p a d -> p (a d)"), x_tiles[T]).then_inc(s_x, 16)

            load_x(0)
            for i in range(NB - 1):
                sp.wait_ge(s_ml, NMB * i + 2 * NMB)
                sp.wait_ge(s_ms, 16 * i + 32)
                sp.dma_start(maps_dram[i], (w_cols[:, 0:MAPS], maps[:].bitcast(F32))[i % 2]).then_inc(s_ms, 16)
            sp.wait_ge(s_ms, 16 * (NB - 1) + 32)
            sp.wait_ge(s_ml, NMB * NB + NMB)
            with sp.Fori(0, 3) as i:
                sp.dma_start(w_raw[:, bass.ds(i * (NX // 3), NX // 3), :], w_moe[:, bass.ds(i * (NX // 3), NX // 3), :]).then_inc(s_wm, 16)
            sp.wait_ge(s_xn[0], 1)
            load_x(1)

            def load_score_maps(i):
                sp.dma_start(maps[:, 0:2 * MAP_A].bitcast(F32), maps_dram[i][:, 0:2 * MAP_A]).then_inc(s_am, 16)

            def load_output_maps(i):
                sp.dma_start(maps[:, 2 * MAP_A:MAPS].bitcast(F32), maps_dram[i][:, 2 * MAP_A:MAPS]).then_inc(s_um, 16)

            def store_combine(T):
                sp.wait_ge(s_cts, T + 2)
                sp.wait_ge(s_cd, 16 * T + 16)
                sp.dma_start(comb_dram[NS:NX, bass.ds(T * P, P)], comb_t[:]).then_inc(s_cd, 16)

            def load_row(B, t, k, first):
                X = NX * B + XT * t + k
                sp.wait_ge(s_g, X + 1)
                if first and k == NS:
                    sp.wait_ge(s_cd, 16 * (TB * B + TB) + 16)
                sp.dma_start(comb_b[:, k % RING, :],
                             comb_dram[XT * t + k, bass.ds(B * BT, BT)].partition_broadcast(P)
                             ).then_inc(s_cb[k % RING], 16)

            def store_block(B):
                sp.wait_ge(s_out, 2 * B + 4)
                sp.dma_start(out_blk[B], x1[:, bass.ds(B % 2, 1), :, :].rearrange("p a t d -> p (a t) d")
                             ).then_inc(s_st, 16)

            def free_residual(B):
                sp.wait_ge(s_st, 16 * B + 16)
                sp.sem_inc(s_x1free, 1)

            def tile_step(B, t, first, flush, tail, main, head, load=False):
                T = TB * (B + 1) + t
                if head:
                    load_x(T + 1)
                for k in range(XT):
                    load_row(B, t, k, first)
                    if load and k == 3:
                        i = B // BLK_B if isinstance(B, int) else sp.snap(B // BLK_B)
                        sp.wait_ge(s_s, 3 * T + 3)
                        load_score_maps(i)
                    if load and k == 7:
                        i = B // BLK_B if isinstance(B, int) else sp.snap(B // BLK_B)
                        sp.wait_ge(s_o, T + 1)
                        load_output_maps(i)
                    if first and k == NS - 1:
                        store_combine(T - 1)
                    if tail and not first and k == 6:
                        store_combine(T - 1)
                    if flush and k == 5:
                        store_block(B - 1)
                    if flush and k == 6:
                        free_residual(B - 1)

            with sp.Fori(1, TB) as t:
                load_x(t + 1)
                store_combine(t - 1)

            def moe_block(B, first_block, attend, go_on, load=False):
                tile_step(B, 0, True, not first_block, True, attend, attend)
                if load:
                    with sp.Fori(1, TB - 1) as t:
                        tile_step(B, t, False, False, True, True, True)
                    tile_step(B, TB - 1, False, False, True, True, True, True)
                elif go_on or not attend:
                    with sp.Fori(1, TB) as t:
                        tile_step(B, t, False, False, attend, attend, attend)
                else:
                    with sp.Fori(1, TB - 1) as t:
                        tile_step(B, t, False, False, True, True, True)
                    tile_step(B, TB - 1, False, False, True, True, False)

            moe_block(0, True, True, True, True)
            with sp.Fori(0, N_BLK // 2 - 2) as i:
                moe_block(2 * i + 1, False, True, True)
                moe_block(2 * i + 2, False, True, True, True)
            moe_block(N_BLK - 3, False, True, True)
            moe_block(N_BLK - 2, False, True, False)
            moe_block(N_BLK - 1, False, False, False)
            store_block(N_BLK - 1)
            sp.wait_ge(s_st, 16 * N_BLK)

        @block.gpsimd
        def _(pool):
            nc.gpsimd.memset(w_cols[:, kv_0:kv_0 + 2 * HJ + 2 * MC * WIN], 0.0)
            pool.drain()
            nc.gpsimd.memset(ones[:], 1.0).then_inc(s_kz, 1)
            pool.drain()
            pool.wait_ge(s_wm, 16 * 3)

            def stage(X, e, k, first_col, hi, lo, s_free, s_lo):
                raw = w_raw[:, bass.ds(e, 1), first_col:first_col + EW].rearrange("p a n -> p (a n)")
                r = k % RING
                pool.wait_ge(s_free, X + 1)
                nc.gpsimd.tensor_tensor(hi[:, r, :], raw, ones[:].broadcast_to([P, EW]), ALU.mult)
                pool.drain()
                nc.gpsimd.tensor_tensor(lo[:, r, :], raw, hi[:, r, :].bitcast(F32), ALU.subtract).then_inc(s_lo, 1)

            for k in range(2):
                stage(k, k, k, 0, wu_hi, wu_lo, s_up, s_wu)
            with pool.Fori(0, N_BLK) as B:
                with pool.Fori(0, TB) as t:
                    for k in range(XT):
                        X = NX * B + XT * t + k
                        ahead = XT * t + k + 2 if k + 2 < XT else (XT * t + k + 2) % NX
                        stage(X + 2, ahead, k + 2, 0, wu_hi, wu_lo, s_up, s_wu)
                        stage(X, XT * t + k, k, EW, wd_hi, wd_lo, s_dn, s_wd)

        @block.scalar
        def _(act):
            act.wait_ge(s_const, 16 * 8)
            nc.scalar.activation(tanh_g[:], gates[:], ACT.Tanh).then_inc(s_tanh, 1)

            def context(b, place):
                for src_0, dst in ((0, k_hi), (2, v_hi)):
                    act.wait_ge(s_kvp, 2 * b + 3 + src_0 // 2)
                    for m in range(MC):
                        src = ps[:, src_0 + m // 3, (m % 3) * J:(m % 3 + 1) * J]
                        for i in range(2):
                            r = slice(i * DH, (i + 1) * DH)
                            o = k_hi[r, 2 * m + i, :] if dst is k_hi else v_hi[r, m, P + i * J:P + (i + 1) * J]
                            ins = nc.scalar.activation(o, src[r, :], ACT.Copy)
                        if m >= 2:
                            ins.then_inc(s_kvh, 1)
                act.wait_ge(s_ms, 16 * b + 16)
                for n, bank in enumerate(MAP_BANKS):
                    at, size = map_columns(n)
                    act.wait_ge(s_mp, NMB * b + n + 1)
                    nc.scalar.activation(place[:, at:at + size], ps[:, bank, 0:size], ACT.Copy).then_inc(s_mh, 1)

            act.wait_ge(s_kz, 1)
            with act.Fori(0, NB // 2) as i:
                context(2 * i, staged)
                context(2 * i + 1, maps)

            act.sem_inc(s_cts, 1)

            def normed_t(T, ln):
                act.wait_ge(s_xt[ln], T + 1)
                if ln == 0:
                    nc.scalar.activation(x1t_hi[:], att[:, 0, 0:EW], ACT.Copy).then_inc(s_xth, 1)
                else:
                    dst = x2t_hi[:, bass.ds(T // TB % 2, 1), :, bass.ds(T % TB * P, P)].rearrange("p a c n -> p (a c) n")
                    nc.scalar.activation(dst, att[:, 2, 0:EW].rearrange("p (c n) -> p c n", c=KC), ACT.Copy)
                    nc.scalar.activation(x2t_f[:], att[:, 2, 0:EW], ACT.Copy).then_inc(s_x2f, 1)

            def exps(T, bank):
                act.wait_ge(s_nm, 3 * T + bank + 1)
                h0 = sum(BANK_H[:bank])
                for i in range(BANK_H[bank]):
                    h = h0 + i
                    ins = nc.scalar.activation(prob[:, h * J:(h + 1) * J], att[:, bank, i * J:(i + 1) * J], ACT.Exp,
                                               bias=nmax[:, h:h + 1], scale=SCALE, accum_out=psum_exp[:, h:h + 1])
                ins.then_inc(s_p, 1)

            def prob_t(T):
                for bank in range(3):
                    n = min(4, NCH - 4 * bank) * P
                    act.wait_ge(s_pt, 3 * T + bank + 1)
                    nc.scalar.activation(pt_hi[:, 512 * bank:512 * bank + n], att[:, bank, 0:n], ACT.Copy).then_inc(s_pth, 1)

            def logits_exp(T):
                act.wait_ge(s_l, T + 1)
                nc.scalar.activation(exp_l[:], att[:, 2, 320:320 + NE], ACT.Exp, scale=-1.0).then_inc(s_e, 1)

            def combine_t(T):
                act.wait_ge(s_ct, T + 1)
                act.wait_ge(s_cd, 16 * T + 16)
                nc.scalar.activation(comb_t[:], att[0:NE, 2, 384:512], ACT.Copy).then_inc(s_cts, 1)

            def hidden_hi(X, k):
                act.wait_ge(s_g, X + 4)
                nc.scalar.activation(act_hi[:, k % RING, :], act_f[:, k % RING, :], ACT.Copy).then_inc(s_gh, 1)

            def hidden(X, k):
                a = act_f[:, k % RING, :]
                act.wait_ge(s_up, X + 4)
                nc.scalar.activation(a, hid[:, k % RING, :], ACT.Relu)
                act.drain()
                nc.scalar.activation(a, a, ACT.Square).then_inc(s_sq, 1)

            def sum_scaled(B):
                act.wait_ge(s_dn, NX * B + NX + 3)
                for c in range(KC):
                    nc.scalar.activation(y_t[:, c, :], acc[:, c, :], ACT.Copy, scale=tanh_g[:, 1:2]).then_inc(s_y, 1)

            def tile_step(B, t, first, flush, tail, main, head):
                T = TB * (B + 1) + t
                for k in range(XT):
                    X = NX * B + XT * t + k
                    if not (first and not flush and k == 0):
                        hidden_hi(X - 1, (k - 1) % RING)
                    if main and k == 1 and not flush:
                        exps(T, 0)
                    hidden(X, k)
                    if flush and k == 1:
                        sum_scaled(B - 1)
                        if main:
                            exps(T, 0)
                    if main and k in (1, 2):
                        exps(T, k)
                    if main and k == 3:
                        prob_t(T)
                    if tail and k == 4:
                        combine_t(T - 1)
                    if head and k == 5:
                        normed_t(T + 1, 0)
                    if main and k == 7:
                        normed_t(T, 1)
                    if main and k == 8:
                        logits_exp(T)

            def lone_tile(t, first):
                for bank in range(3):
                    exps(t, bank)
                prob_t(t)
                normed_t(t + 1, 0)
                if not first:
                    combine_t(t - 1)
                normed_t(t, 1)
                logits_exp(t)

            normed_t(0, 0)
            lone_tile(0, True)
            with act.Fori(1, TB) as t:
                lone_tile(t, False)

            def moe_block(B, first_block, attend, go_on):
                tile_step(B, 0, True, not first_block, True, attend, attend)
                if go_on or not attend:
                    with act.Fori(1, TB) as t:
                        tile_step(B, t, False, False, attend, attend, attend)
                else:
                    with act.Fori(1, TB - 1) as t:
                        tile_step(B, t, False, False, True, True, True)
                    tile_step(B, TB - 1, False, False, True, True, False)

            moe_block(0, True, True, True)
            with act.Fori(0, N_BLK // 2 - 2) as i:
                moe_block(2 * i + 1, False, True, True)
                moe_block(2 * i + 2, False, True, True)
            moe_block(N_BLK - 3, False, True, True)
            moe_block(N_BLK - 2, False, True, False)
            moe_block(N_BLK - 1, False, False, False)
            hidden_hi(NX * N_BLK - 1, (NX - 1) % RING)
            sum_scaled(N_BLK - 1)

        @block.vector
        def _(dve):
            V = nc.vector
            half = CD - P
            V.memset(raw_a[half:P, INNER:2 * INNER], 0.0)
            V.memset(raw_b[half:P, INNER:2 * INNER], 0.0)
            V.memset(ctx_raw[half:P, :, 1, :], 0.0)
            V.memset(mask_u8[:], 1)
            V.memset(prob[:, HJ:NCH * P], 0.0)
            V.memset(comb[:], 0.0)
            V.memset(row0[:], 0.0)
            dve.drain()
            V.memset(row0[0:1, :], 1.0)
            V.memset(ones_row, 1.0).then_inc(s_ones, 1)
            dve.drain()
            V.memset(nmax[:], 0.0).then_inc(s_zero, 1)
            dve.sem_inc(s_g, 3)
            dve.sem_inc(s_x1, 2)
            dve.sem_inc(s_ml, NMB)
            dve.sem_inc(s_out, 2)

            def split(dst_hi, dst_lo, raw):
                V.tensor_copy(dst_hi, raw)
                dve.drain()
                return V.tensor_tensor(dst_lo, raw, dst_hi.bitcast(F32), ALU.subtract)

            dve.wait_ge(s_wa, 16 * 8)
            split(wk_hi, wk_lo, raw_a[:, 0:2 * INNER]).then_inc(s_split, 1)
            split(ctx_hi, ctx_lo, ctx_raw[:, 0, :, :]).then_inc(s_win, 1)
            split(wv_hi, wv_lo, raw_b[:, 0:2 * INNER]).then_inc(s_split, 1)
            split(wq_hi, wq_lo, raw_c[:, 0:MC * D])
            split(wo_hi, wo_lo, raw_c[:, MC * D:2 * MC * D]).then_inc(s_split, 1)
            dve.wait_ge(s_const, 16 * 8)
            V.tensor_scalar(mask_add[:], mask_u8[:], -1.0, BIG, ALU.add, ALU.mult).then_inc(s_mask, 1)

            def context(b, place, more):
                for src_0, hi in ((0, k_hi), (2, v_hi)):
                    for m in range(MC):
                        src = ps[:, src_0 + m // 3, (m % 3) * J:(m % 3 + 1) * J]
                        if m in (0, 3):
                            dve.wait_ge(s_kvh, 4 * b + src_0 + m // 3 + 1)
                        for i in range(2):
                            r = slice(i * DH, (i + 1) * DH)
                            if hi is k_hi:
                                h, l = k_hi[r, 2 * m + i, :], k_lo[r, 2 * m + i, :]
                            else:
                                h, l = [a[r, m, P + i * J:P + (i + 1) * J] for a in (v_hi, v_lo)]
                            ins = V.tensor_tensor(l, src[r, :], h.bitcast(F32), ALU.subtract)
                        if m >= 2:
                            ins.then_inc(s_kvl, 1)
                if more:
                    split(ctx_hi, ctx_lo, ctx_raw[:, bass.ds(b + 1, 1), :, :].rearrange("p a c j -> p (a c) j")
                          ).then_inc(s_win, 1)
                for n, bank in enumerate(MAP_BANKS):
                    at, size = map_columns(n)
                    low = at + (MAP_A if n < 6 else MAP_U)
                    dve.wait_ge(s_mh, NMB * b + n + 1)
                    V.tensor_tensor(place[:, low:low + size], ps[:, bank, 0:size],
                                    place[:, at:at + size].bitcast(F32), ALU.subtract).then_inc(s_ml, 1)

            for b in range(NB):
                context(b, (staged, maps)[b % 2], b < NB - 1)

            st, mv = ln_s[:, 0:6], ln_s[:, 6:8]
            ve, y, a, half = ln_s[:, 8:9], ln_s[:, 9:10], ln_s[:, 10:11], ln_s[:, 11:12]

            def norm_stats(src):
                V.bn_stats(st, src)
                dve.drain()
                V.bn_aggr(mv, st)
                dve.drain()
                V.tensor_scalar(ve, mv[:, 1:2], EPS, None, ALU.add)
                V.tensor_scalar(half, mv[:, 1:2], EPS, -0.5, ALU.add, ALU.mult)
                dve.drain()
                V.tensor_scalar(ln_i[:, 0:1], ve.bitcast(I32), 1, None, ALU.logical_shift_right)
                dve.drain()
                V.tensor_scalar(y.bitcast(I32), ln_i[:, 0:1], -1.0, RSQRT_MAGIC, ALU.mult, ALU.add)
                dve.drain()

            def norm_apply(ln, src, dst):
                for _ in range(3):
                    V.scalar_tensor_tensor(a, y, half, y, ALU.mult, ALU.mult)
                    dve.drain()
                    V.scalar_tensor_tensor(y, a, 1.5, y, ALU.add, ALU.mult)
                    dve.drain()
                V.tensor_scalar(dst, src, mv[:, 0:1], y, ALU.subtract, ALU.mult).then_inc(s_xn[ln], 1)

            def half_of_x(T):
                return x_in[:, bass.ds(T % 2, 1), :].rearrange("p a d -> p (a d)")

            def residual_of(T):
                return x1[:, bass.ds(T // TB % 2, 1), bass.ds(T % TB, 1), :].rearrange("p a t d -> p (a t d)")

            def norm_in(T):
                dve.wait_ge(s_x, 16 * T + 16)
                norm_stats(half_of_x(T))
                norm_apply(0, half_of_x(T), x_n1[:])

            def normed_t(T, ln):
                dve.wait_ge((s_xth, s_x2f)[ln], T + 1)
                if ln == 0:
                    V.tensor_tensor(x1t_lo[:], att[:, 0, 0:EW], x1t_hi[:].bitcast(F32), ALU.subtract).then_inc(s_xtl[ln], 1)
                else:
                    par, col = T // TB % 2, T % TB * P
                    hi = x2t_hi[:, bass.ds(par, 1), :, bass.ds(col, P)].rearrange("p a c n -> p (a c) n")
                    lo = x2t_lo[:, bass.ds(par, 1), :, bass.ds(col, P)].rearrange("p a c n -> p (a c) n")
                    V.tensor_tensor(lo, att[:, 2, 0:EW].rearrange("p (c n) -> p c n", c=KC), hi.bitcast(F32),
                                    ALU.subtract).then_inc(s_xtl[ln], 1)

            def maxima(T):
                h = 0
                for bank, nh in enumerate(BANK_H):
                    dve.wait_ge(s_s, 3 * T + bank + 1)
                    V.tensor_reduce(rsum[:, h:h + nh], att[:, bank, 0:nh * J].rearrange("p (a j) -> p a j", a=nh),
                                    op=ALU.max, axis=AX_X)
                    dve.drain()
                    V.tensor_scalar(nmax[:, h:h + nh], rsum[:, h:h + nh], -SCALE, None, ALU.mult).then_inc(s_nm, 1)
                    h += nh

            def normalise(T):
                dve.wait_ge(s_p, 3 * T + 3)
                V.reciprocal(rsum[:], psum_exp[:])
                dve.drain()
                p3 = prob[:, 0:HJ].rearrange("p (h j) -> p h j", h=NH)
                V.tensor_tensor(p3, p3, rsum[:].unsqueeze(2).broadcast_to([P, NH, J]), ALU.mult).then_inc(s_pn, 1)

            def prob_t(T):
                for bank in range(3):
                    n = min(4, NCH - 4 * bank) * P
                    dve.wait_ge(s_pth, 3 * T + bank + 1)
                    V.tensor_tensor(pt_lo[:, 512 * bank:512 * bank + n], att[:, bank, 0:n],
                                    pt_hi[:, 512 * bank:512 * bank + n].bitcast(F32), ALU.subtract).then_inc(s_ptl, 1)

            def residual(T, blk):
                dve.wait_ge(s_o, T + 1)
                dve.wait_ge(s_x1free, blk)
                V.tensor_tensor(x_n2, att[:, 1, 0:D], bias_o[:], ALU.add)
                dve.drain()
                V.scalar_tensor_tensor(residual_of(T), x_n2, tanh_g[:, 0:1], half_of_x(T), ALU.mult, ALU.add).then_inc(s_x1, 1)

            def norm_out_stats(T):
                dve.drain()
                norm_stats(residual_of(T))

            def norm_out(T):
                norm_apply(1, residual_of(T), x_n2)

            best, idx_g = grp[:, 56:64], grp[:, 64:72]
            low = grp[:, 48:56]

            def router_groups(T):
                dve.wait_ge(s_e, T + 1)
                V.tensor_scalar(score[:], exp_l[:], 1.0, None, ALU.add)
                dve.drain()
                V.reciprocal(score[:], score[:])
                dve.drain()
                V.tensor_tensor(biased[:], score[:], bias_e[:], ALU.add)
                dve.drain()
                mx, mn = grp[:, 0:16], grp[:, 16:32]
                V.tensor_tensor(mx, biased[:, 0:NE:2], biased[:, 1:NE:2], ALU.max)
                V.tensor_tensor(mn, biased[:, 0:NE:2], biased[:, 1:NE:2], ALU.min)
                dve.drain()
                first, other = grp[:, 32:40], grp[:, 40:48]
                V.tensor_tensor(first, mx[:, 0:16:2], mx[:, 1:16:2], ALU.max)
                V.tensor_tensor(other, mx[:, 0:16:2], mx[:, 1:16:2], ALU.min)
                V.tensor_tensor(low, mn[:, 0:16:2], mn[:, 1:16:2], ALU.max)
                dve.drain()
                V.tensor_tensor(other, other, low, ALU.max)
                dve.drain()
                V.tensor_tensor(first, first, other, ALU.add)
                dve.drain()

            def router_masked():
                first = grp[:, 32:40]
                V.max(best, first)
                dve.drain()
                V.max_index(grp_i[:, 0:8], best, first)
                dve.drain()
                V.tensor_copy(idx_g, grp_i[:, 0:8])
                dve.drain()
                V.tensor_tensor(hot_g[:], iota_f[:, 0:NG].unsqueeze(1).broadcast_to([P, TOPG, NG]),
                                idx_g[:, 0:TOPG].unsqueeze(2).broadcast_to([P, TOPG, NG]), ALU.is_equal)
                dve.drain()
                V.tensor_reduce(low, hot_g[:].rearrange("p k g -> p g k"), op=ALU.max, axis=AX_X)
                dve.drain()
                V.tensor_tensor(masked[:].rearrange("p (g e) -> p g e", g=NG), biased[:].rearrange("p (g e) -> p g e", g=NG),
                                low.unsqueeze(2).broadcast_to([P, NG, GE]), ALU.mult)
                dve.drain()
                V.tensor_scalar(masked[:], masked[:], 0.0, None, ALU.add)
                dve.drain()

            def router_weights():
                V.max(best, masked[:])
                dve.drain()
                V.max_index(grp_i[:, 8:16], best, masked[:])
                dve.drain()
                V.tensor_copy(idx_g, grp_i[:, 8:16])
                dve.drain()
                V.tensor_tensor(hot[:], iota_f[:].unsqueeze(1).broadcast_to([P, TOPK, NE]),
                                idx_g[:, 0:TOPK].unsqueeze(2).broadcast_to([P, TOPK, NE]), ALU.is_equal)
                dve.drain()
                V.tensor_reduce(sel[:], hot[:].rearrange("p k e -> p e k"), op=ALU.max, axis=AX_X)
                dve.drain()
                total = grp[:, 72:73]
                V.tensor_tensor_reduce(out=weighted[:], in0=sel[:], in1=score[:], scale=1.0, scalar=0.0,
                                       op0=ALU.mult, op1=ALU.add, accum_out=total)
                dve.drain()
                V.tensor_scalar(total, total, 1e-20, None, ALU.add)
                dve.drain()
                V.reciprocal(total, total)
                dve.drain()
                V.tensor_scalar(comb[:, 0:NE], weighted[:], total, ROUTED_SCALE, ALU.mult, ALU.mult).then_inc(s_c, 1)

            def hidden_lo(X, k):
                r = k % RING
                dve.wait_ge(s_gh, X + 1)
                V.tensor_tensor(act_lo[:, r, :], act_f[:, r, :], act_hi[:, r, :].bitcast(F32), ALU.subtract).then_inc(s_gl, 1)

            def hidden(X, B, t, k):
                r = k % RING
                dve.wait_ge(s_sq, X + 1)
                dve.wait_ge(s_cb[r], 16 * ((NX // RING) * B + (XT // RING) * t + k // RING + 1))
                V.tensor_tensor(act_f[:, r, :], act_f[:, r, :], comb_b[:, r, :], ALU.mult).then_inc(s_g, 1)

            def add_sum(B):
                for j in range(2):
                    dst = x1[:, bass.ds(B % 2, 1), 2 * j:2 * j + 2, :].rearrange("p a t d -> p (a t d)")
                    dve.wait_ge(s_yt, 2 * B + j + 1)
                    V.tensor_tensor(dst, acc[:, j, :], dst, ALU.add).then_inc(s_out, 1)

            def tile_step(B, t, first, flush, tail, main, head):
                T = TB * (B + 1) + t
                for k in range(XT):
                    X = NX * B + XT * t + k
                    if not (first and not flush and k == 0):
                        hidden_lo(X - 1, (k - 1) % RING)
                    if head and k == 4:
                        norm_in(T + 1)
                    hidden(X, B, t, k)
                    if flush and k == 1:
                        add_sum(B - 1)
                    if k == 0:
                        if tail:
                            router_groups(T - 1)
                        if main:
                            maxima(T)
                    if tail and k == 1:
                        router_masked()
                    if main and k == 2:
                        normalise(T)
                    if tail and k == 2:
                        router_weights()
                    if main and k == 3:
                        prob_t(T)
                    if main and k == 4:
                        residual(T, B + 1)
                    if head and k == 5:
                        normed_t(T + 1, 0)
                    if main and k == 5:
                        norm_out_stats(T)
                    if main and k == 6:
                        norm_out(T)
                    if main and k == 7:
                        normed_t(T, 1)

            def lone_tile(t, first):
                maxima(t)
                if not first:
                    router_groups(t - 1)
                normalise(t)
                if not first:
                    router_masked()
                prob_t(t)
                norm_in(t + 1)
                if not first:
                    router_weights()
                residual(t, 1)
                normed_t(t + 1, 0)
                norm_out_stats(t)
                norm_out(t)
                normed_t(t, 1)

            dve.wait_ge(s_tanh, 1)
            norm_in(0)
            normed_t(0, 0)
            lone_tile(0, True)
            with dve.Fori(1, TB) as t:
                lone_tile(t, False)

            def moe_block(B, first_block, attend, go_on):
                tile_step(B, 0, True, not first_block, True, attend, attend)
                if go_on or not attend:
                    with dve.Fori(1, TB) as t:
                        tile_step(B, t, False, False, attend, attend, attend)
                else:
                    with dve.Fori(1, TB - 1) as t:
                        tile_step(B, t, False, False, True, True, True)
                    tile_step(B, TB - 1, False, False, True, True, False)

            moe_block(0, True, True, True)
            with dve.Fori(0, N_BLK // 2 - 2) as i:
                moe_block(2 * i + 1, False, True, True)
                moe_block(2 * i + 2, False, True, True)
            moe_block(N_BLK - 3, False, True, True)
            moe_block(N_BLK - 2, False, True, False)
            moe_block(N_BLK - 1, False, False, False)
            hidden_lo(NX * N_BLK - 1, (NX - 1) % RING)
            add_sum(N_BLK - 1)

        @block.tensor
        def _(pe):
            pe.sem_inc(s_up, 3)
            pe.sem_inc(s_dn, 3)
            pe.sem_inc(s_kvp, 2)
            pe.wait_ge(s_kz, 1)
            with pe.Fori(0, NB) as b:
                pe.wait_ge(s_win, b + 1)
                pe.wait_ge(s_ml, NMB * b + NMB)
                for bank_0, w_hi, w_lo, n_split in ((0, wk_hi, wk_lo, 1), (2, wv_hi, wv_lo, 2)):
                    pe.wait_ge(s_split, n_split)
                    for m in range(MC):
                        for c in range(2):
                            w = slice(c * INNER + m * P, c * INNER + (m + 1) * P)
                            ins = three(ps[:, bank_0 + m // 3, (m % 3) * J:(m % 3 + 1) * J], w_hi[:, w], w_lo[:, w],
                                        ctx_hi[:, c, :], ctx_lo[:, c, :], c == 0, c == 1)
                    ins.then_inc(s_kvp, 1)
                pe.wait_ge(s_split, 3)
                pe.wait_ge(s_kvl, 4 * b + 2)
                for n in range(6):
                    c, h0, nh = n // 3, sum(BANK_H[:n % 3]), BANK_H[n % 3]
                    for h in range(h0, h0 + nh):
                        w = slice(h // 2 * D + c * P, h // 2 * D + (c + 1) * P)
                        ins = three(ps[:, MAP_BANKS[n], (h - h0) * J:(h - h0 + 1) * J], wq_hi[:, w], wq_lo[:, w],
                                    k_hi[:, h, :], k_lo[:, h, :], True, True)
                    ins.then_inc(s_mp, 1)
                pe.wait_ge(s_kvl, 4 * b + 4)
                for c in range(NCH):
                    bank = MAP_BANKS[6 + c // 2]
                    if c == 4:
                        pe.wait_ge(s_ml, NMB * b + NMB + 3)
                    pairs = [m for m, ch in AV if ch == c]
                    for m in pairs:
                        at = P + c * P - 2 * m * J
                        w = slice(m * D, (m + 1) * D)
                        ins = three(ps[:, bank, c % 2 * D:(c % 2 + 1) * D], v_hi[:, m, at:at + P], v_lo[:, m, at:at + P],
                                    wo_hi[:, w], wo_lo[:, w], m == pairs[0], m == pairs[-1])
                    if c % 2:
                        ins.then_inc(s_mp, 1)
            pe.wait_ge(s_ml, NMB * NB + NMB)
            pe.wait_ge(s_mask, 1)

            def normed_t(T, ln):
                x_n = (x_n1, x_n2)[ln]
                pe.wait_ge(s_xn[ln], T + 1)
                if ln == 1:
                    pe.wait_ge(s_cts, T + 1)
                for c in range(KC):
                    ins = nc.tensor.transpose(att[:, 2 * ln, c * P:(c + 1) * P], x_n[:, c * P:(c + 1) * P], ident[:])
                ins.then_inc(s_xt[ln], 1)

            def scores(T, b):
                pe.wait_ge(s_xtl[0], T + 1)
                h0 = 0
                for bank, nh in enumerate(BANK_H):
                    if bank == 2 and not (isinstance(T, int) and T == 0):
                        pe.wait_ge(s_e, T)
                    nc.tensor.matmul(att[:, bank, 0:nh * J].rearrange("p (a j) -> p a j", a=nh), row0[:],
                                     mask_add[:, bass.ds(b, 1), :].broadcast_to([P, nh, J]),
                                     start=True, stop=False, skip_group_check=True)
                    n = slice(h0 * J, (h0 + nh) * J)
                    for c in range(KC):
                        f = slice(c * P, (c + 1) * P)
                        ins = three(att[:, bank, 0:nh * J], x1t_hi[:, f], x1t_lo[:, f], a_hi[:, c, n], a_lo[:, c, n], False, c == KC - 1)
                    ins.then_inc(s_s, 1)
                    h0 += nh

            def prob_t(T):
                pe.wait_ge(s_pn, T + 1)
                for c in range(NCH):
                    ins = nc.tensor.transpose(att[:, c // 4, c % 4 * P:(c % 4 + 1) * P], prob[:, c * P:(c + 1) * P], ident[:])
                    if c % 4 == 3 or c == NCH - 1:
                        ins.then_inc(s_pt, 1)

            def attn_out(T):
                pe.wait_ge(s_ptl, 3 * T + 3)
                for c in range(NCH):
                    r = slice(c * P, (c + 1) * P)
                    ins = three(att[:, 1, 0:D], pt_hi[:, r], pt_lo[:, r], u_hi[:, c, :], u_lo[:, c, :], c == 0, c == NCH - 1)
                ins.then_inc(s_o, 1)

            def logits(T):
                pe.wait_ge(s_xtl[1], T + 1)
                for c in range(KC):
                    ins = nc.tensor.matmul(att[:, 2, 320:320 + NE], x2t_f[:, c * P:(c + 1) * P], gate_w[:, c, :],
                                           start=c == 0, stop=c == KC - 1, skip_group_check=True)
                ins.then_inc(s_l, 1)

            def combine_t(T):
                pe.wait_ge(s_c, T + 1)
                pe.wait_ge(s_cts, T + 1)
                nc.tensor.transpose(att[:, 2, 384:512], comb[:], ident[:]).then_inc(s_ct, 1)

            def up(X, B, k):
                r = k % RING
                pe.wait_ge(s_wu, X + 1)
                for c in range(KC):
                    w = slice(c * P, (c + 1) * P)
                    hi = x2t_hi[:, bass.ds(B % 2, 1), c, :].rearrange("p a n -> p (a n)")
                    lo = x2t_lo[:, bass.ds(B % 2, 1), c, :].rearrange("p a n -> p (a n)")
                    ins = three(hid[:, r, :], wu_hi[:, r, w], wu_lo[:, r, w], hi, lo, c == 0, c == KC - 1)
                ins.then_inc(s_up, 1)

            def down(X, k, start, stop):
                r = k % RING
                pe.wait_ge(s_wd, X + 1)
                pe.wait_ge(s_gl, X + 1)
                for c in range(KC):
                    w = slice(c * P, (c + 1) * P)
                    ins = three(acc[:, c, :], wd_hi[:, r, w], wd_lo[:, r, w], act_hi[:, r, :], act_lo[:, r, :], start, stop)
                ins.then_inc(s_dn, 1)

            def loads_before(B):
                return 16 * ((B + 1) // BLK_B)

            def sum_t(B):
                pe.wait_ge(s_y, 2 * B + 2)
                for i in range(TB):
                    for c in range(KC):
                        ins = nc.tensor.transpose(acc[:, i // 2, i % 2 * D + c * P:i % 2 * D + (c + 1) * P],
                                                  y_t[:, c, i * P:(i + 1) * P], ident[:])
                    if i % 2:
                        ins.then_inc(s_yt, 1)

            def tile_step(B, t, first, flush, tail, main, head):
                T = TB * (B + 1) + t
                for k in range(XT):
                    X = NX * B + XT * t + k
                    up(X, B, k)
                    if flush and k == 2:
                        sum_t(B - 1)
                        pe.wait_ge(s_out, 2 * B + 2)
                    if not first or flush or k >= 2:
                        down(X - 2, (k - 2) % RING, first and k == 2, first and k == 1)
                    if main and k == 0:
                        if first and not (isinstance(B, int) and B == 0):
                            pe.wait_ge(s_am, loads_before(B))
                        scores(T, (B + 1) // BLK_B)
                    if main and k == 3:
                        prob_t(T)
                    if main and k == 4:
                        if first and not (isinstance(B, int) and B == 0):
                            pe.wait_ge(s_um, loads_before(B))
                        pe.wait_ge(s_ptl, 3 * T + 3)
                    if tail and k == 4:
                        combine_t(T - 1)
                    if main and k == 4:
                        attn_out(T)
                    if head and k == 5:
                        normed_t(T + 1, 0)
                    if main and k == 7:
                        normed_t(T, 1)
                    if main and k == 8:
                        logits(T)

            def lone_tile(t, first):
                scores(t, 0)
                prob_t(t)
                attn_out(t)
                normed_t(t + 1, 0)
                if not first:
                    combine_t(t - 1)
                normed_t(t, 1)
                logits(t)

            normed_t(0, 0)
            lone_tile(0, True)
            with pe.Fori(1, TB) as t:
                lone_tile(t, False)

            def moe_block(B, first_block, attend, go_on):
                pe.wait_ge(s_xtl[1], TB * B + TB)
                tile_step(B, 0, True, not first_block, True, attend, attend)
                if go_on or not attend:
                    with pe.Fori(1, TB) as t:
                        tile_step(B, t, False, False, attend, attend, attend)
                else:
                    with pe.Fori(1, TB - 1) as t:
                        tile_step(B, t, False, False, True, True, True)
                    tile_step(B, TB - 1, False, False, True, True, False)

            moe_block(0, True, True, True)
            with pe.Fori(0, N_BLK // 2 - 2) as i:
                moe_block(2 * i + 1, False, True, True)
                moe_block(2 * i + 2, False, True, True)
            moe_block(N_BLK - 3, False, True, True)
            moe_block(N_BLK - 2, False, True, False)
            moe_block(N_BLK - 1, False, False, False)
            for e in (NX - 2, NX - 1):
                down(NX * (N_BLK - 1) + e, e, False, e == NX - 1)
            sum_t(N_BLK - 1)


_INS = ["x", "ctx_t", "mask", "g_xattn", "g_ffn", "w_qt", "w_k", "w_v", "w_o", "b_o", "gate_t", "e_bias",
        "w_moe", "eye", "iota"]


def kernel(x, ctx_768, mask_BxS2_bk0, g_xattn, g_ffn, L0_xattn_W_q, L0_xattn_W_k, L0_xattn_W_v, L0_xattn_W_o,
           L0_xattn_b_o, L0_ffn_gate_w, L0_ffn_e_bias, L0_ffn_up_w, L0_ffn_down_w, L0_ffn_shared_up_w,
           L0_ffn_shared_down_w):
    import numpy as np
    import concourse.bacc as bacc
    from concourse.bass_utils import run_bass_kernel_spmd

    x = np.asarray(x)
    shape = x.shape
    d = shape[-1]
    up, down = np.asarray(L0_ffn_up_w), np.asarray(L0_ffn_down_w)
    part = up.shape[1]
    sup = np.asarray(L0_ffn_shared_up_w).reshape(-1, part, d)
    sdn = np.asarray(L0_ffn_shared_down_w).reshape(d, -1, part).transpose(1, 0, 2)
    ups = np.concatenate([sup, up])
    downs = np.concatenate([sdn, down])
    ups = ups.transpose(2, 0, 1).reshape(d // P, P, -1, part).transpose(1, 2, 0, 3).reshape(P, -1, d)
    downs = downs.transpose(2, 0, 1)
    arrays = {
        "x": x.reshape(-1, d),
        "ctx_t": np.roll(np.asarray(ctx_768), -1, axis=0).transpose(0, 2, 1),
        "mask": np.asarray(mask_BxS2_bk0),
        "g_xattn": np.asarray(g_xattn), "g_ffn": np.asarray(g_ffn),
        "w_qt": np.asarray(L0_xattn_W_q).T, "w_k": np.asarray(L0_xattn_W_k), "w_v": np.asarray(L0_xattn_W_v),
        "w_o": np.asarray(L0_xattn_W_o), "b_o": np.asarray(L0_xattn_b_o),
        "gate_t": np.asarray(L0_ffn_gate_w).T, "e_bias": np.asarray(L0_ffn_e_bias),
        "w_moe": np.concatenate([ups, downs], axis=2),
        "eye": np.eye(P, dtype=np.float32),
        "iota": np.tile(np.arange(len(L0_ffn_gate_w), dtype=np.float32), (P, 1)),
    }
    nc = bacc.Bacc("TRN2", target_bir_lowering=False, num_devices=1)
    feeds, args = {}, []
    for name in _INS:
        a = np.ascontiguousarray(arrays[name])
        feeds[f"in_{name}"] = a
        args.append(nc.dram_tensor(f"in_{name}", a.shape, mybir.dt.from_np(a.dtype), kind="ExternalInput").ap())
    out = nc.dram_tensor("out", arrays["x"].shape, F32, kind="ExternalOutput").ap()
    flamingo_block(nc, *args, out)
    r = run_bass_kernel_spmd(nc, [feeds], core_ids=[0])
    return r.results[0]["out"].reshape(shape)
```
